# Optimizing a Trainium2 kernel written in Bass

```python
import numpy as np
import jax
import jax.numpy as jnp

def _softmax(x, axis=-1):
    return jax.nn.softmax(x, axis=axis)
def _gelu(x):
    return jax.nn.gelu(x, approximate=True)
def _silu(x):
    return jax.nn.silu(x)
def _sigmoid(x):
    return jax.nn.sigmoid(x)
def _layernorm(x, axis=-1, eps=1e-5):
    m = jnp.mean(x, axis=axis, keepdims=True)
    v = jnp.var(x, axis=axis, keepdims=True)
    return (x - m) / jnp.sqrt(v + eps)
def _scatter_add(tgt, idx, src, axis=0):
    return tgt.at[idx].add(src)
def _segment_sum(src, seg, n):
    return jax.ops.segment_sum(src, seg, n)

kernel_name = 'mk_conv_preact_d2_conv_nchw16_35c695'

def setup_inputs(seed: int = 0):
    np.random.seed(seed)
    _w = jnp.asarray
    def _rec_inputs():
        import jax
        import jax.numpy as jnp
        _gk = jax.random.key(seed)
        x = -0.000125 + 0.9999 * jax.random.normal(jax.random.fold_in(_gk, 1), (8, 16, 512, 512), jnp.float32)
        return x
    x = _rec_inputs()
    def _L0_conv_setup():
        import jax, jax.numpy as jnp
        import numpy as np
        from jax import lax
        B, C, O, K, H, W = (8, 16, 16, 3, 512, 512)
        STRIDE, PAD = (1, 1)
        BN_EPS = 1e-05

        def _forward(x, w_fft_real, w_fft_imag, rot_w, rot_b, bn_gamma, bn_beta):
            z = jnp.einsum('bchw,oc->bohw', x, rot_w) + rot_b[None, :, None, None]
            mu = jnp.mean(z, axis=(0, 2, 3), keepdims=True)
            var = jnp.mean((z - mu) ** 2, axis=(0, 2, 3), keepdims=True)
            z = (z - mu) * lax.rsqrt(var + BN_EPS)
            z = z * bn_gamma[None, :, None, None] + bn_beta[None, :, None, None]
            angles = jnp.mean(z, axis=(2, 3))
            angle = jnp.sum(angles, axis=1, keepdims=True)
            angle = jnp.tanh(angle) * (jnp.pi / 4)
            cos_theta = jnp.cos(angle)[:, 0]
            freq = jnp.fft.fftfreq(K).astype(jnp.float32)
            fx, fy, fz = jnp.meshgrid(freq, freq, freq, indexing='ij')
            fsum = fx + fy + fz
            phase = jnp.exp(-2j * jnp.pi * (cos_theta[:, None, None, None] * fsum))
            w_fft = w_fft_real + 1j * w_fft_imag
            w_rot = w_fft[None] * phase[:, None, None]
            rotated = jnp.fft.ifftn(w_rot, axes=(-3, -2, -1)).real
            mid = K // 2
            w2d = rotated[:, :, :, mid, :, :]
            gw = w2d.reshape(B * O, C, K, K)
            xg = x.reshape(1, B * C, H, W)
            out = lax.conv_general_dilated(xg, gw, window_strides=(STRIDE, STRIDE), padding=[(PAD, PAD), (PAD, PAD)], feature_group_count=B, dimension_numbers=('NCHW', 'OIHW', 'NCHW'))
            return out.reshape(B, O, out.shape[2], out.shape[3])
        key = jax.random.key(seed)
        ks = jax.random.split(key, 5)
        std = float(np.sqrt(2.0 / (O * K ** 3)))
        return {'x': jax.random.normal(ks[0], (B, C, H, W), jnp.float32), 'w_fft_real': jax.random.normal(ks[1], (O, C, K, K, K), jnp.float32) * std, 'w_fft_imag': jax.random.normal(ks[2], (O, C, K, K, K), jnp.float32) * std, 'rot_w': jax.random.normal(ks[3], (3, C), jnp.float32) * float(np.sqrt(1.0 / C)), 'rot_b': jnp.zeros((3,), jnp.float32), 'bn_gamma': jnp.ones((3,), jnp.float32), 'bn_beta': jnp.zeros((3,), jnp.float32)}
    _L0_conv_all = _L0_conv_setup()
    _L0_conv_in = {k: v for k, v in _L0_conv_all.items() if k in ('w_fft_real', 'w_fft_imag', 'rot_w', 'rot_b', 'bn_gamma', 'bn_beta', )}
    del _L0_conv_all

    def _L1_conv_setup():
        import jax, jax.numpy as jnp
        import numpy as np
        K_SIZE = 3
        PAD = K_SIZE // 2

        def _diag_L(n, k):
            half = k // 2
            d = np.zeros(n, dtype=np.float32)
            d[:half] = 1.0
            d[n - half:] = 1.0
            if 2 * half < k:
                d[half] = 1.0
            return d

        def _circular_pad(w, H, W, k, p):
            w = jnp.roll(jnp.pad(jnp.flip(w, -1), ((0, 0), (0, 0), (0, 0), (0, W - k))), -p, axis=-1)
            w = jnp.roll(jnp.pad(jnp.flip(w, -2), ((0, 0), (0, 0), (0, H - k), (0, 0))), -p, axis=-2)
            return w
        key = jax.random.key(seed)
        kx, kw = jax.random.split(key)
        x = jax.random.normal(kx, (16, 16, 256, 256), dtype=jnp.float32)
        weight = jax.random.normal(kw, (16, 16, 3, 3), dtype=jnp.float32) * (2.0 / (16 * 9)) ** 0.5
        return {'x': x, 'weight': weight}
    _L1_conv_all = _L1_conv_setup()
    _L1_conv_in = {k: v for k, v in _L1_conv_all.items() if k in ('weight', )}
    del _L1_conv_all

    return {
        "x": x,
        "L0_conv_w_fft_real": _L0_conv_in["w_fft_real"],
        "L0_conv_w_fft_imag": _L0_conv_in["w_fft_imag"],
        "L0_conv_rot_w": _L0_conv_in["rot_w"],
        "L0_conv_rot_b": _L0_conv_in["rot_b"],
        "L0_conv_bn_gamma": _L0_conv_in["bn_gamma"],
        "L0_conv_bn_beta": _L0_conv_in["bn_beta"],
        "L1_conv_weight": _L1_conv_in["weight"],
    }

def reference(x, L0_conv_w_fft_real, L0_conv_w_fft_imag, L0_conv_rot_w, L0_conv_rot_b, L0_conv_bn_gamma, L0_conv_bn_beta, L1_conv_weight):
    import jax
    import jax.numpy as jnp
    def _L0_conv_ref(x, w_fft_real, w_fft_imag, rot_w, rot_b, bn_gamma, bn_beta):
        import jax, jax.numpy as jnp
        import numpy as np
        from jax import lax
        B, C, O, K, H, W = (8, 16, 16, 3, 512, 512)
        STRIDE, PAD = (1, 1)
        BN_EPS = 1e-05

        def _forward(x, w_fft_real, w_fft_imag, rot_w, rot_b, bn_gamma, bn_beta):
            z = jnp.einsum('bchw,oc->bohw', x, rot_w) + rot_b[None, :, None, None]
            mu = jnp.mean(z, axis=(0, 2, 3), keepdims=True)
            var = jnp.mean((z - mu) ** 2, axis=(0, 2, 3), keepdims=True)
            z = (z - mu) * lax.rsqrt(var + BN_EPS)
            z = z * bn_gamma[None, :, None, None] + bn_beta[None, :, None, None]
            angles = jnp.mean(z, axis=(2, 3))
            angle = jnp.sum(angles, axis=1, keepdims=True)
            angle = jnp.tanh(angle) * (jnp.pi / 4)
            cos_theta = jnp.cos(angle)[:, 0]
            freq = jnp.fft.fftfreq(K).astype(jnp.float32)
            fx, fy, fz = jnp.meshgrid(freq, freq, freq, indexing='ij')
            fsum = fx + fy + fz
            phase = jnp.exp(-2j * jnp.pi * (cos_theta[:, None, None, None] * fsum))
            w_fft = w_fft_real + 1j * w_fft_imag
            w_rot = w_fft[None] * phase[:, None, None]
            rotated = jnp.fft.ifftn(w_rot, axes=(-3, -2, -1)).real
            mid = K // 2
            w2d = rotated[:, :, :, mid, :, :]
            gw = w2d.reshape(B * O, C, K, K)
            xg = x.reshape(1, B * C, H, W)
            out = lax.conv_general_dilated(xg, gw, window_strides=(STRIDE, STRIDE), padding=[(PAD, PAD), (PAD, PAD)], feature_group_count=B, dimension_numbers=('NCHW', 'OIHW', 'NCHW'))
            return out.reshape(B, O, out.shape[2], out.shape[3])
        return _forward(x, w_fft_real, w_fft_imag, rot_w, rot_b, bn_gamma, bn_beta)

    def _L1_conv_ref(x, weight):
        import jax, jax.numpy as jnp
        import numpy as np
        K_SIZE = 3
        PAD = K_SIZE // 2

        def _diag_L(n, k):
            half = k // 2
            d = np.zeros(n, dtype=np.float32)
            d[:half] = 1.0
            d[n - half:] = 1.0
            if 2 * half < k:
                d[half] = 1.0
            return d

        def _circular_pad(w, H, W, k, p):
            w = jnp.roll(jnp.pad(jnp.flip(w, -1), ((0, 0), (0, 0), (0, 0), (0, W - k))), -p, axis=-1)
            w = jnp.roll(jnp.pad(jnp.flip(w, -2), ((0, 0), (0, 0), (0, H - k), (0, 0))), -p, axis=-2)
            return w
        B, Ci, H, W = x.shape
        k, p = (K_SIZE, PAD)
        w_pad = _circular_pad(weight, H, W, k, p)
        dL = jnp.asarray(np.outer(_diag_L(H, k), _diag_L(W, k)))
        Lw = jnp.fft.fft2(w_pad * dL)
        Kx = jnp.fft.ifft2(x, norm='ortho')
        z = jnp.einsum('oihw,bihw->bohw', Lw, Kx)
        y = jnp.fft.fft2(z, norm='ortho')
        return jnp.real(y).astype(x.dtype)

    def _gn(v, G=8, eps=1e-5):
        B_, C_, H_, W_ = v.shape
        g = v.reshape(B_, G, C_ // G, H_, W_)
        m = jnp.mean(g, axis=(2, 3, 4), keepdims=True)
        s = jnp.var(g, axis=(2, 3, 4), keepdims=True)
        return ((g - m) / jnp.sqrt(s + eps)).reshape(v.shape)

    def _ln_c(v, eps=1e-6):
        m = jnp.mean(v, axis=1, keepdims=True)
        s = jnp.var(v, axis=1, keepdims=True)
        return (v - m) / jnp.sqrt(s + eps)

    def _ln_t(v, eps=1e-5):
        m = jnp.mean(v, axis=-1, keepdims=True)
        s = jnp.var(v, axis=-1, keepdims=True)
        return (v - m) / jnp.sqrt(s + eps)

    def _to_tokens(v):
        B_, C_, H_, W_ = v.shape
        return v.reshape(B_, C_, H_ * W_).transpose(0, 2, 1)
    def _from_tokens(t, like):
        B_, C_, H_, W_ = like.shape
        return t.transpose(0, 2, 1).reshape(B_, C_, H_, W_)

    x = x + _L0_conv_ref(_gn(x), L0_conv_w_fft_real, L0_conv_w_fft_imag, L0_conv_rot_w, L0_conv_rot_b, L0_conv_bn_gamma, L0_conv_bn_beta)
    x = x + _L1_conv_ref(_gn(x), L1_conv_weight)
    return x


_drawn_inputs = setup_inputs


def setup_inputs(seed=0):
    import zlib

    import numpy as np

    out = dict(_drawn_inputs(seed))
    spreads = {'L0_conv_rot_b': (0.0, 0.1), 'L0_conv_bn_gamma': (1.0, 0.6), 'L0_conv_bn_beta': (0.0, 2.0)}
    factors = {'L0_conv_rot_w': 64.0}
    for name, (base, spread) in spreads.items():
        noise = np.random.default_rng([zlib.crc32(name.encode()), seed]).standard_normal(out[name].shape)
        drawn = base * np.exp(spread * noise) if base else spread * noise
        out[name] = jnp.asarray(drawn.astype(out[name].dtype))
    for name, factor in factors.items():
        out[name] = (out[name] * factor).astype(out[name].dtype)
    return out
```

```python
from contextlib import ExitStack

import concourse.bass as bass
from concourse import mybir

F32 = mybir.dt.float32
F16 = mybir.dt.float16
ALU = mybir.AluOpType
ACT = mybir.ActivationFunctionType
AX = mybir.AxisListType

B, C, H, W = 8, 16, 512, 512
P = 128
NPIX = H * W
GROUP = 2
K3 = 27
PITCH = W // 2 + 1
TROWS = H // 4 + 1
FOUT = TROWS * PITCH
FIN = (TROWS + 1) * PITCH + 1
CH = 2048
NFULL = FOUT // CH
NCH = NFULL + 1
TAIL = FOUT - NFULL * CH
HALO = PITCH + 1
WIN = CH + HALO
TWIN = TAIL + HALO
ROWS_CH = 8
LEAD = 8
GN_EPS, BN_EPS = 1e-5, 1e-5
YS = 16.0
WS = 64.0

PXP = NPIX // P
ACHUNK = 4096
NACH = PXP * C // ACHUNK
ASLOTS = 4

_COLS = [("mask_g", 128), ("fold", 16), ("gm", 128), ("rep", 128), ("pair", 16), ("id16", 16),
         ("ones", 128), ("id0", 256), ("id1", 256), ("pmask", 2), ("row0", 1), ("rown", 1),
         ("u", 9), ("v", 9), ("cm", 4), ("sm", 3)]
COL = {}
_at = 0
for _n, _w in _COLS:
    COL[_n] = (_at, _at + _w)
    _at += _w
NCONST = _at


def conv_program(nc, x_pix, x_tiles, wf, rotw, small, w1band, consts, out):
    ctx = ExitStack()
    with ctx:
        def sb(name, shape, dt=F32):
            return ctx.enter_context(nc.sbuf_tensor(name, shape, dt))

        def sem(name):
            return ctx.enter_context(nc.semaphore(name))

        img = sb("img", [P, LEAD + FIN + 1])
        xy = sb("xy", [P, 2, WIN])
        nat = sb("nat", [P, 2, 2, WIN], F16)
        shf = sb("shf", [P, 2, 2, CH + 2], F16)
        wc = sb("wc", [P, 2, 2, 2, 2, 64], F16)
        cst = sb("cst", [P, NCONST])
        w32 = sb("w32", [P, 256])
        w132 = sb("w132", [P, 256])
        wtmp = sb("wtmp", [P, 256])
        stats = sb("stats", [P, (4 * NFULL + 1) * 6])
        gnp = sb("gnp", [P, 3, B])
        cur = sb("cur", [P, 2, 3])
        sm = sb("sm", [P, 32])
        smallp = sb("smallp", [P, 9])
        rw = sb("rw", [C, 3])
        wfs = sb("wfs", [2 * K3, 256])
        zc = sb("zc", [P, 320])
        zt = sb("zt", [2 * K3, 9 * B])
        zero = sb("zero", [P, 16], F16)
        zerof = sb("zerof", [P, PITCH])
        ps = ctx.enter_context(nc.psum_tensor("ps", [P, 8, 512], F32))

        taps = nc.dram_tensor("taps_scratch", [B, C, 5, 5, C], F32).ap()
        bands = nc.dram_tensor("bands_scratch", [B, P, 256], F32).ap()

        apix = img[:, 0:ASLOTS * ACHUNK].rearrange("p (s n) -> p s n", s=ASLOTS)
        o = ASLOTS * ACHUNK
        psums = img[:, o:o + B * NACH * C].rearrange("p (b j c) -> p b j c", b=B, j=NACH)
        o += B * NACH * C
        gmask = img[:, o:o + B * P].rearrange("p (b q) -> p b q", b=B)
        o += B * P
        sumc = img[:, o:o + B * C].rearrange("p (b c) -> p b c", b=B)
        o += B * C
        gram = img[0:C, o:o + B * C].rearrange("p (b c) -> p b c", b=B)
        o += B * C
        band0 = img[:, o:o + B * 256].rearrange("p (b m) -> p b m", b=B)
        o += B * 256
        tapsb = img[0:9 * B, o:o + 256]
        o += 256
        zpad = img[:, o:o + 400]

        def c(name, parts=P):
            a, z = COL[name]
            return cst[0:parts, a:z]

        const_in = sem("const_in")
        primed = sem("primed")
        a_in = [sem(f"a_in{s}") for s in range(ASLOTS)]
        a_gram = sem("a_gram")
        a_sum = sem("a_sum")
        a_zero = sem("a_zero")
        a_mask = sem("a_mask")
        zpe = sem("zpe")
        zve = sem("zve")
        zac = sem("zac")
        zdma = sem("zdma")
        dve_step = sem("dve_step")
        x_in = [sem(f"x_in{s}") for s in range(2)]
        w_in = sem("w_in")
        y_ready = sem("y_ready")
        hi_ready = sem("hi_ready")
        lo_ready = sem("lo_ready")
        shf_in = [sem(f"shf_in{s}") for s in range(2)]
        w_ready = sem("w_ready")
        pe_done = sem("pe_done")
        evac_done = sem("evac_done")
        st_in = sem("st_in")
        st_pe = sem("st_pe")
        st_var = sem("st_var")
        st_std = sem("st_std")
        out_done = [sem(f"out_done{s}") for s in range(2)]

        passed = sem("passed")

        def hold(eng, signal, value):
            eng.wait_ge(signal, value)
            eng.sem_inc(passed, 1)

        block = ctx.enter_context(nc.Block())

        STEPS = 2 * NCH

        def step(b, layer, n):
            return b * STEPS + layer * NCH + n

        def slot(layer, n_parity):
            return (layer * NCH + n_parity) % 2

        def uses(b, layer, i):
            return b * NCH + i + (0 if layer == 0 else None)

        def chunk_use(b, layer, i, r):
            if layer == 0:
                return b * NCH + i
            return b * NCH + i + (NFULL // 2 if r == 0 else NFULL // 2 + 1)

        @block.sync
        def _(sp):
            for dst, src in ((cst[:, :], consts), (rw[:, :], rotw), (smallp[:, :], small),
                             (wfs[:, :], wf), (w132[:, :], w1band)):
                sp.dma_start(dst, src).then_inc(const_in, 16)
            with sp.Fori(0, B) as b:
                with sp.Fori(0, NACH // ASLOTS) as jj:
                    for s in range(ASLOTS):
                        k = b * NACH + jj * ASLOTS + s
                        hold(sp, a_gram, k + 1)
                        hold(sp, a_sum, k + 1)
                        sp.dma_start(apix[:, s, :], x_pix[b, :, bass.ds((jj * ASLOTS + s) * ACHUNK, ACHUNK)]
                                     ).then_inc(a_in[s], 16)
            hold(sp, zve, Z_ZPAD)
            sp.dma_start(taps.rearrange("b c p q o -> (b c) (p q o)"), zpad).then_inc(zdma, 16)
            hold(sp, zdma, 16)
            hold(sp, zve, Z_TAPS)
            for t in range(9):
                sp.dma_start(taps[:, :, 1 + t // 3, 1 + t % 3, :],
                             tapsb[t * B:(t + 1) * B, :].rearrange("p (c o) -> p c o", c=C)).then_inc(zdma, 16)
            hold(sp, zdma, 16 * 10)
            n = 10
            for half in range(2):
                for r in range(2):
                    for ci in range(2):
                        g = ((half * 2 + r) * 2 + ci) * C
                        for kind in range(2):
                            row = 2 * (half if kind == 0 else 1 - half) + r
                            for dj in range(2):
                                cc = 2 * dj + ci
                                for a in range(2):
                                    m = ((kind * 2 + dj) * 2 + a) * 32
                                    src = taps[:, :, row + a, cc:cc + 2, :].rearrange("b c q o -> c b (q o)")
                                    sp.dma_start(band0[g:g + C, :, m:m + 32], src).then_inc(zdma, 16)
                                    n += 1
            hold(sp, zdma, 16 * n)
            sp.dma_start(bands.rearrange("b p m -> p b m"), band0).then_inc(zdma, 16)
            hold(sp, zdma, 16 * (n + 1))

            def load_x(b, i, r, lo, n, width=WIN):
                hold(sp, lo_ready, lo)
                sp.dma_start(xy[:, r, 0:width], x_tiles[b, :, bass.ds(n * CH, width)]).then_inc(x_in[r], 16)

            def make_shifted(t, s, width=CH + 1):
                hold(sp, lo_ready, t + 1 + 2)
                hold(sp, pe_done, t + 1)
                sp.dma_start(shf[64:128, s, :, 0:width], nat[64:128, s, :, 0:width]).then_inc(shf_in[s], 16)
                sp.dma_start(shf[0:64, s, :, 0:width], nat[0:64, s, :, PITCH:PITCH + width]
                             ).then_inc(shf_in[s], 16)

            def store(b, t, i, r, n, width=CH):
                hold(sp, evac_done, t + 1 + 2)
                hold(sp, out_done[r], 16 * (b * (NFULL // 2 + 1 - r) + i + NFULL // 2 + 1))
                sp.dma_start(out[b, :, bass.ds(n * CH, width)], img[:, bass.ds(LEAD + n * CH, width)]
                             ).then_inc(out_done[r], 16)

            with sp.Fori(0, B) as b:
                hold(sp, w_ready, 2 * b + 1)
                sp.dma_start(w32[:, :], bands[b]).then_inc(w_in, 16)
                t0 = step(b, 0, 0)
                load_x(b, 0, 0, t0 + 1, 0)
                load_x(b, 0, 1, t0 + 2, 1)
                with sp.Fori(0, NFULL // 2 - 1) as i:
                    for r in range(2):
                        n = i * 2 + r
                        make_shifted(t0 + n, r)
                        load_x(b, i, r, t0 + n + 3, n + 2)
                i = NFULL // 2 - 1
                make_shifted(t0 + NFULL - 2, 0)
                load_x(b, i, 0, t0 + NFULL + 1, NFULL, TWIN)
                make_shifted(t0 + NFULL - 1, 1)
                make_shifted(t0 + NFULL, 0, TAIL + 1)
                t1 = step(b, 1, 0)
                for r in range(2):
                    make_shifted(t1 + r, slot(1, r))
                with sp.Fori(1, NFULL // 2) as i:
                    for r in range(2):
                        n = i * 2 + r
                        make_shifted(t1 + n, slot(1, r))
                        store(b, t1 + n - 2, i - 1, r, n - 2)
                make_shifted(t1 + NFULL, slot(1, 0), TAIL + 1)
                store(b, t1 + NFULL - 2, NFULL // 2 - 1, 0, NFULL - 2)
                store(b, t1 + NFULL - 1, NFULL // 2 - 1, 1, NFULL - 1)
                store(b, t1 + NFULL, NFULL // 2, 0, NFULL, TAIL)
            hold(sp, out_done[0], 16 * ((B + 1) * (NFULL // 2 + 1)))
            hold(sp, out_done[1], 16 * (B * (NFULL // 2) + NFULL // 2 + 1))

        @block.tensor
        def _(pe):
            pe.sem_inc(a_gram, ASLOTS)
            pe.sem_inc(pe_done, 2)
            pe.wait_ge(a_zero, 1)
            with pe.Fori(0, B // 2) as bb:
                for h in range(2):
                    b = bb * 2 + h
                    acc = ps[:, h, 0:P]
                    pe.wait_ge(a_mask, b + 1)
                    nc.tensor.matmul(acc, zerof[:, 0:P], zerof[:, 0:P], start=True, stop=False)
                    with pe.Fori(0, NACH // ASLOTS) as jj:
                        for s in range(ASLOTS):
                            pe.wait_ge(a_in[s], 16 * (b * (NACH // ASLOTS) + jj + 1))
                            for q in range(ACHUNK // P):
                                blk = apix[:, s, q * P:(q + 1) * P]
                                mm = nc.tensor.matmul(acc, blk, blk, start=False, stop=False)
                            mm.then_inc(a_gram, 1)
                    nc.tensor.matmul(acc, zerof[:, 0:P], zerof[:, 0:P], start=False, stop=True).then_inc(zpe, 1)
            done = B

            def mm(out_, lhs, rhs, last=True):
                m = nc.tensor.matmul(out_, lhs, rhs, start=True, stop=True)
                if last:
                    m.then_inc(zpe, 1)

            pe.wait_ge(const_in, 16 * 5)
            pe.wait_ge(zve, Z_SUMS)
            for h in range(2):
                mm(ps[0:C, 2 + h, 0:512], c("fold"), gmask[:, 4 * h:4 * h + 4, :].rearrange("p b q -> p (b q)"), False)
            for b in range(B):
                mm(ps[0:C, 4, b:b + 1], sumc[:, b, :], c("ones")[:, 0:1], b == B - 1)
            pe.wait_ge(zve, Z_MOM)
            mm(ps[0:C, 4, 16:32], c("pair", C), zc[0:C, 0:16])
            pe.wait_ge(zve, Z_WA)
            for b in range(B):
                mm(ps[0:C, 4, 64 + 3 * b:67 + 3 * b], gram[:, b, :], zc[0:C, 72 + 3 * b:75 + 3 * b], b == B - 1)
            pe.wait_ge(zve, Z_FORMS)
            mm(ps[:, 5, 0:72], c("ones", C), zc[0:C, 96:168], False)
            mm(ps[:, 5, 128:152], c("rep", C), zc[0:C, 40:64])
            pe.wait_ge(zve, Z_T)
            mm(ps[0:9 * B, 6, 0:256], zt[:, :], wfs[:, :])

            def chunk(t, layer, s, width=None):
                banks = [(q, 512) for q in range(4)] if width is None else [(0, width)]
                pe.wait_ge(lo_ready, t + 1 + 2)
                pe.wait_ge(evac_done, t + 1)
                return banks

            def matmuls(layer, s, banks):
                for q, w in banks:
                    k = 0
                    for whl, xhl in ((0, 0), (1, 0), (0, 1)):
                        for dj in range(2):
                            for kind, tiles in ((0, nat), (1, shf)):
                                last = nc.tensor.matmul(
                                    ps[64 * kind:64 * kind + 64, 4 * s + q, 0:w], wc[:, layer, whl, kind, dj, :],
                                    tiles[:, s, xhl, q * 512 + dj:q * 512 + dj + w], start=(k == 0), stop=(k == 5))
                            k += 1
                last.then_inc(pe_done, 1)

            with pe.Fori(0, B) as b:
                for layer in range(2):
                    if layer == 1:
                        pe.wait_ge(st_in, b + 1)
                        nc.tensor.matmul(ps[:, 4, 0:2], c("gm"), sm[:, 2:4], start=True, stop=True).then_inc(st_pe, 1)
                    hold(pe, w_ready, 2 * b + layer + 2)
                    with pe.Fori(0, NFULL // 2) as i:
                        for r in range(2):
                            t = step(b, layer, 0) + i * 2 + r
                            s = slot(layer, r)
                            banks = chunk(t, layer, s)
                            pe.wait_ge(shf_in[s], 32 * (chunk_use(b, layer, i, r) + 1))
                            matmuls(layer, s, banks)
                    t = step(b, layer, NFULL)
                    s = slot(layer, 0)
                    banks = chunk(t, layer, s, TAIL)
                    pe.wait_ge(shf_in[s], 32 * (chunk_use(b, layer, NFULL // 2, 0) + 1))
                    matmuls(layer, s, banks)

        @block.scalar
        def _(act):
            act.sem_inc(evac_done, 2)
            act.wait_ge(zve, Z_VAR)
            nc.scalar.activation(zc[0:C, 64:72], zc[0:C, 32:40], ACT.Sqrt).then_inc(zac, 1)
            act.wait_ge(zve, Z_BNVAR)
            nc.scalar.activation(zc[:, 176:179], zc[:, 172:175], ACT.Sqrt).then_inc(zac, 1)
            act.wait_ge(zve, Z_ANGLE)
            nc.scalar.activation(zc[:, 232:240], zc[:, 224:232], ACT.Tanh).then_inc(zac, 1)
            act.wait_ge(zve, Z_COSARG)
            nc.scalar.activation(zc[:, 248:256], zc[:, 240:248], ACT.Sin).then_inc(zac, 1)
            act.wait_ge(zve, Z_PHASE)
            nc.scalar.activation(zc[:, 272:288], zc[:, 256:272], ACT.Sin).then_inc(zac, 1)

            def round_hi(t, s, width=WIN):
                act.wait_ge(y_ready, t + 1)
                act.wait_ge(pe_done, t + 1)
                nc.scalar.activation(nat[:, s, 0, 0:width], xy[:, s, 0:width], ACT.Identity).then_inc(hi_ready, 1)

            def evacuate(t, layer, s, n, width=None):
                act.wait_ge(pe_done, t + 1 + 2)
                if width is None:
                    src, width = ps[:, 4 * s:4 * s + 4, :].rearrange("p a b -> p (a b)"), CH
                else:
                    src = ps[:, 4 * s, 0:width]
                nc.scalar.activation(img[:, bass.ds(LEAD + n * CH, width)], src, ACT.Identity,
                                     bias=cur[:, layer, 0:1], scale=1.0 / (YS * WS)).then_inc(evac_done, 1)

            with act.Fori(0, B) as b:
                for layer in range(2):
                    t0 = step(b, layer, 0)

                    def stored(i, r):
                        if layer == 0:
                            act.wait_ge(out_done[r], 16 * (b * (NFULL // 2 + 1 - r) + i + 1))

                    for r in range(2):
                        round_hi(t0 + r, slot(layer, r))
                    with act.Fori(1, NFULL // 2) as i:
                        for r in range(2):
                            n = i * 2 + r
                            round_hi(t0 + n, slot(layer, r))
                            stored(i - 1, r)
                            evacuate(t0 + n - 2, layer, slot(layer, r), n - 2)
                    round_hi(t0 + NFULL, slot(layer, 0), TWIN)
                    for r in range(2):
                        stored(NFULL // 2 - 1, r)
                        evacuate(t0 + NFULL - 2 + r, layer, slot(layer, r), NFULL - 2 + r)
                    stored(NFULL // 2, 0)
                    evacuate(t0 + NFULL, layer, slot(layer, 0), NFULL, TAIL)
                    if layer == 0:
                        act.wait_ge(st_var, b + 1)
                        nc.scalar.activation(sm[:, 8:9], sm[:, 7:8], ACT.Sqrt).then_inc(st_std, 1)

        @block.vector
        def _(ve):
            V = nc.vector
            ve.sem_inc(a_sum, ASLOTS)
            ve.sem_inc(a_mask, 2)
            ve.sem_inc(lo_ready, 2)
            ve.sem_inc(w_ready, 1)
            ve.sem_inc(out_done[0], 16 * (NFULL // 2 + 1))
            ve.sem_inc(out_done[1], 16 * (NFULL // 2 + 1))
            V.memset(zero[:, :], 0.0)
            V.memset(zerof[:, :], 0.0).then_inc(a_zero, 1)
            ve.wait_ge(const_in, 16 * 5)
            with ve.Fori(0, B // 2) as bb:
                for h in range(2):
                    b = bb * 2 + h
                    with ve.Fori(0, NACH // ASLOTS) as jj:
                        for s in range(ASLOTS):
                            ve.wait_ge(a_in[s], 16 * (b * (NACH // ASLOTS) + jj + 1))
                            V.tensor_reduce(psums[:, b, bass.ds(jj * ASLOTS + s, 1), :].rearrange("p j c -> p (j c)"),
                                            apix[:, s, :].rearrange("p (k c) -> p c k", c=C),
                                            AX.X, ALU.add).then_inc(a_sum, 1)
                    ve.wait_ge(zpe, b + 1)
                    V.tensor_tensor(gmask[:, bass.ds(b, 1), :].rearrange("p b q -> p (b q)"), ps[:, h, 0:P],
                                    c("mask_g"), ALU.mult).then_inc(a_mask, 1)

            count = [0]

            def link(ins):
                count[0] += 1
                ins.then_inc(zve, 1)
                ve.wait_ge(zve, count[0])
                return count[0]

            pe_steps = [B]
            act_steps = [0]

            def after_pe():
                pe_steps[0] += 1
                ve.wait_ge(zpe, pe_steps[0])

            def after_act():
                act_steps[0] += 1
                ve.wait_ge(zac, act_steps[0])

            def at(k, n):
                assert k == n, (k, n)

            at(link(V.memset(zpad, 0.0)), Z_ZPAD)
            ve.wait_ge(a_mask, B + 2)
            ve.wait_ge(a_sum, B * NACH + ASLOTS)
            at(link(V.tensor_reduce(sumc, psums.rearrange("p b j c -> p b c j"), AX.X, ALU.add)), Z_SUMS)
            after_pe()
            for hh in range(2):
                link(V.tensor_reduce(gram[:, 4 * hh:4 * hh + 4, :],
                                     ps[0:C, 2 + hh, :].rearrange("p (b k c) -> p b c k", b=4, k=8),
                                     AX.X, ALU.add))
            link(V.tensor_scalar(gram, gram, 1.0 / NPIX, None, ALU.mult))
            link(V.tensor_scalar(zc[0:C, 0:8], ps[0:C, 4, 0:8], 1.0 / NPIX, None, ALU.mult))
            for b in range(B):
                link(V.tensor_tensor(zc[0:C, 296:312], gram[:, b, :], c("id16", C), ALU.mult))
                n = link(V.tensor_reduce(zc[0:C, 8 + b:9 + b], zc[0:C, 296:312], AX.X, ALU.add))
            at(n, Z_MOM)
            after_pe()
            gmean, var, std, inv = zc[0:C, 40:48], zc[0:C, 32:40], zc[0:C, 64:72], zc[0:C, 16:24]
            tmp = zc[0:C, 24:32]
            link(V.tensor_copy(gmean, ps[0:C, 4, 16:24]))
            link(V.tensor_tensor(tmp, gmean, gmean, ALU.mult))
            link(V.tensor_tensor(var, ps[0:C, 4, 24:32], tmp, ALU.subtract))
            at(link(V.tensor_scalar(var, var, GN_EPS, None, ALU.add)), Z_VAR)

            def newton(inv, std, var, tmp):
                link(V.reciprocal(inv, std))
                link(V.tensor_tensor(tmp, inv, inv, ALU.mult))
                link(V.tensor_tensor(tmp, tmp, var, ALU.mult))
                link(V.tensor_scalar(tmp, tmp, -0.5, 1.5, ALU.mult, ALU.add))
                link(V.tensor_tensor(inv, inv, tmp, ALU.mult))

            after_act()
            newton(inv, std, var, tmp)
            link(V.tensor_scalar(zc[0:C, 48:56], inv, YS, None, ALU.mult))
            link(V.tensor_tensor(tmp, inv, var, ALU.mult))
            link(V.tensor_scalar(zc[0:C, 56:64], tmp, WS, None, ALU.mult))
            wa = zc[0:C, 72:96].rearrange("p (b o) -> p b o", o=3)
            for k in range(3):
                n = link(V.tensor_scalar(wa[:, :, k], inv, rw[:, k:k + 1], None, ALU.mult))
            at(n, Z_WA)
            forms = zc[0:C, 96:168].rearrange("p (f b o) -> p f b o", f=3, o=3)
            link(V.tensor_tensor(tmp, zc[0:C, 0:8], gmean, ALU.subtract))
            for k in range(3):
                link(V.tensor_tensor(forms[:, 1, :, k], wa[:, :, k], zc[0:C, 0:8], ALU.mult))
                link(V.tensor_tensor(forms[:, 2, :, k], wa[:, :, k], tmp, ALU.mult))
            after_pe()
            at(link(V.tensor_tensor(zc[0:C, 96:120], zc[0:C, 72:96], ps[0:C, 4, 64:88], ALU.mult)), Z_FORMS)
            after_pe()
            q = zc[:, 96:168]
            link(V.tensor_copy(q, ps[:, 5, 0:72]))
            link(V.tensor_copy(gnp[:, :, :], ps[:, 5, 128:152].rearrange("p (f b) -> p f b", f=3)))
            qz, qm, qs = q[:, 0:24], q[:, 24:48], q[:, 48:72]

            def bo(a):
                return a.rearrange("p (b o) -> p b o", o=3)

            def ob(a):
                return a.rearrange("p (b o) -> p o b", o=3)

            link(V.tensor_tensor(qm, qm, qm, ALU.mult))
            link(V.tensor_tensor(qz, qz, qm, ALU.subtract))
            for k in range(3):
                link(V.tensor_scalar(bo(qs)[:, :, k], bo(qs)[:, :, k], smallp[:, k:k + 1], None, ALU.add))
            zm = zc[:, 168:171]
            link(V.tensor_reduce(zm, ob(qs), AX.X, ALU.add))
            link(V.tensor_scalar(zm, zm, 1.0 / B, None, ALU.mult))
            for k in range(3):
                link(V.tensor_scalar(bo(qs)[:, :, k], bo(qs)[:, :, k], zm[:, k:k + 1], None, ALU.subtract))
            link(V.tensor_tensor(qm, qs, qs, ALU.mult))
            link(V.tensor_tensor(qz, qz, qm, ALU.add))
            bv = zc[:, 172:175]
            link(V.tensor_reduce(bv, ob(qz), AX.X, ALU.add))
            at(link(V.tensor_scalar(bv, bv, 1.0 / B, BN_EPS, ALU.mult, ALU.add)), Z_BNVAR)
            after_act()
            bi = zc[:, 180:183]
            newton(bi, zc[:, 176:179], bv, zc[:, 184:187])
            link(V.tensor_tensor(bi, bi, smallp[:, 3:6], ALU.mult))
            for k in range(3):
                link(V.tensor_scalar(bo(qs)[:, :, k], bo(qs)[:, :, k], bi[:, k:k + 1], smallp[:, 6 + k:7 + k],
                                     ALU.mult, ALU.add))
            at(link(V.tensor_reduce(zc[:, 224:232], bo(qs), AX.X, ALU.add)), Z_ANGLE)
            after_act()
            pi = 3.141592653589793
            at(link(V.tensor_scalar(zc[:, 240:248], zc[:, 232:240], pi / 4, pi / 2, ALU.mult, ALU.add)), Z_COSARG)
            after_act()
            link(V.tensor_scalar(zc[:, 256:264], zc[:, 248:256], 2 * pi / 3, None, ALU.mult))
            at(link(V.tensor_scalar(zc[:, 264:272], zc[:, 248:256], -2 * pi / 3, pi / 2, ALU.mult, ALU.add)), Z_PHASE)
            after_act()
            s1, c1 = zc[:, 272:280], zc[:, 280:288]
            s2, c2, s3, c3 = zc[:, 192:200], zc[:, 200:208], zc[:, 208:216], zc[:, 216:224]
            t8 = zc[:, 288:296]
            link(V.tensor_tensor(s2, s1, c1, ALU.mult))
            link(V.tensor_scalar(s2, s2, 2.0, None, ALU.mult))
            link(V.tensor_tensor(c2, c1, c1, ALU.mult))
            link(V.tensor_scalar(c2, c2, 2.0, -1.0, ALU.mult, ALU.add))
            link(V.tensor_tensor(s3, s2, c1, ALU.mult))
            link(V.tensor_tensor(t8, c2, s1, ALU.mult))
            link(V.tensor_tensor(s3, s3, t8, ALU.add))
            link(V.tensor_tensor(c3, c2, c1, ALU.mult))
            link(V.tensor_tensor(t8, s2, s1, ALU.mult))
            link(V.tensor_tensor(c3, c3, t8, ALU.subtract))
            n2 = 2 * K3
            cf, sf = zc[0:n2, 96:104], zc[0:n2, 104:112]
            cm, smk = c("cm", n2), c("sm", n2)
            link(V.tensor_scalar(cf, c1[0:n2, :], cm[:, 1:2], cm[:, 0:1], ALU.mult, ALU.add))
            link(V.scalar_tensor_tensor(cf, c2[0:n2, :], cm[:, 2:3], cf, ALU.mult, ALU.add))
            link(V.scalar_tensor_tensor(cf, c3[0:n2, :], cm[:, 3:4], cf, ALU.mult, ALU.add))
            link(V.tensor_scalar(sf, s1[0:n2, :], smk[:, 0:1], None, ALU.mult))
            link(V.scalar_tensor_tensor(sf, s2[0:n2, :], smk[:, 1:2], sf, ALU.mult, ALU.add))
            link(V.scalar_tensor_tensor(sf, s3[0:n2, :], smk[:, 2:3], sf, ALU.mult, ALU.add))
            for k in range(9):
                link(V.tensor_scalar(zt[:, 8 * k:8 * k + 8], cf, c("u", n2)[:, k:k + 1], None, ALU.mult))
                n = link(V.scalar_tensor_tensor(zt[:, 8 * k:8 * k + 8], sf, c("v", n2)[:, k:k + 1],
                                                zt[:, 8 * k:8 * k + 8], ALU.mult, ALU.add))
            at(n, Z_T)
            after_pe()
            at(link(V.tensor_copy(tapsb, ps[0:9 * B, 6, 0:256])), Z_TAPS)
            V.tensor_scalar(w132[:, :], w132[:, :], WS, None, ALU.mult).then_inc(dve_step, 1)
            ve.wait_ge(zdma, 16 * (10 + 64 + 1))
            V.memset(img[:, :], 0.0).then_inc(dve_step, 1)
            ve.wait_ge(dve_step, 2)

            PER_IMAGE = 3 + NCH + (NCH + 2) + 4 + 4 + 3 + 7 + 2
            mark = [0]
            base = [2]

            def chain(ins, b):
                mark[0] += 1
                ins.then_inc(dve_step, 1)
                ve.wait_ge(dve_step, b * PER_IMAGE + mark[0] + base[0])

            def weights(b, layer, w):
                chain(V.scalar_tensor_tensor(wtmp[:, :], c("id0" if layer == 0 else "id1"), cur[:, layer, 2:3], w,
                                             ALU.mult, ALU.add), b)
                hi = wc[:, layer, 0].rearrange("p a b m -> p (a b m)")
                lo = wc[:, layer, 1].rearrange("p a b m -> p (a b m)")
                chain(V.tensor_copy(hi, wtmp[:, :]), b)
                V.tensor_tensor(lo, wtmp[:, :], hi, ALU.subtract).then_inc(w_ready, 1)

            def normalize(dst, src, layer):
                return V.tensor_scalar(dst, src, cur[:, layer, 0:1], cur[:, layer, 1:2], ALU.subtract, ALU.mult)

            def split_lo(t, s, width=WIN):
                ve.wait_ge(hi_ready, t + 1)
                V.tensor_tensor(nat[:, s, 1, 0:width], xy[:, s, 0:width], nat[:, s, 0, 0:width],
                                ALU.subtract).then_inc(lo_ready, 1)

            def y_of_x(b, t, i, r, phase, width=WIN, rows=ROWS_CH + 1):
                n0 = b * (NFULL // 2 + 1 - r) + i + 1
                ve.wait_ge(x_in[r], 16 * n0)
                ins = normalize(xy[:, r, 0:width], xy[:, r, 0:width], 0)
                return ins

            def count_step(b, steps_before):
                ve.wait_ge(dve_step, b * PER_IMAGE + steps_before + base[0])

            NY = 3
            NM = NY + NCH

            def bn_chunk(b, n, t, order, width=CH, rows=ROWS_CH, first=False, last=False):
                ve.wait_ge(evac_done, t + 1 + 2)
                if first or last:
                    at_ = LEAD + (0 if first else FOUT - PITCH)
                    V.tensor_scalar(img[:, at_:at_ + PITCH], img[:, at_:at_ + PITCH],
                                    c("row0" if first else "rown"), None, ALU.mult).then_inc(dve_step, 1)
                    ve.wait_ge(dve_step, b * PER_IMAGE + base[0] + order[0])
                    order = order[1:]
                pairs = img[:, bass.ds(LEAD - 1 + n * (ROWS_CH * PITCH), rows * PITCH)].rearrange(
                    "p (k s) -> p k s", s=PITCH)[:, :, 0:2]
                V.tensor_tensor(pairs, pairs, c("pmask").unsqueeze(1).to_broadcast([P, rows, 2]),
                                ALU.mult).then_inc(dve_step, 1)
                ve.wait_ge(dve_step, b * PER_IMAGE + base[0] + order[0])
                for k in range((width + 511) // 512):
                    w = min(512, width - 512 * k)
                    ins = V.bn_stats(stats[:, bass.ds((n * 4 + k) * 6, 6)],
                                     img[:, bass.ds(LEAD + n * CH + 512 * k, w)])
                if last:
                    ins.then_inc(dve_step, 1)

            with ve.Fori(0, B) as b:
                mark[0] = 0
                chain(V.tensor_copy(cur[:, 0, :], gnp[:, :, bass.ds(b, 1)].rearrange("p f b -> p (f b)")), b)
                ve.wait_ge(w_in, 16 * (b + 1))
                weights(b, 0, w32[:, :])
                t0 = step(b, 0, 0)
                k = 3

                def y0(b, t, n, i, r, k, width=WIN, rows=ROWS_CH + 1, first=False, last=False):
                    y_of_x(b, t, i, r, None, width).then_inc(dve_step, 1)
                    ve.wait_ge(dve_step, b * PER_IMAGE + base[0] + k)
                    if first:
                        V.tensor_copy(xy[:, r, 1:PITCH], zerof[:, 1:PITCH])
                    if last:
                        V.tensor_copy(xy[:, r, TAIL + 1:TAIL + PITCH], zerof[:, 1:PITCH])
                    edge = xy[:, r, bass.ds(n * ROWS_CH, (rows - 1) * PITCH + 1)]
                    edge = edge[:, 0:(rows - 1) * PITCH + 1:PITCH]
                    V.tensor_copy(edge, zero[:, 0:rows]).then_inc(y_ready, 1)

                for n in range(4):
                    k += 1
                    y0(b, t0 + n, n, n // 2, n % 2, k, first=(n == 0))
                    if n == 3:
                        bn_chunk(b, 0, t0, [k + 1, k + 2], first=True)
                        k += 2
                    split_lo(t0 + n, n % 2)
                kk = k
                with ve.Fori(2, NFULL // 2) as i:
                    for r in range(2):
                        n = i * 2 + r
                        y0(b, t0 + n, n, i, r, kk + (i - 2) * 4 + 2 * r + 1)
                        bn_chunk(b, n - 3, t0 + n - 3, [kk + (i - 2) * 4 + 2 * r + 2])
                        split_lo(t0 + n, r)
                k = kk + 4 * (NFULL // 2 - 2)
                k += 1
                y0(b, t0 + NFULL, NFULL, NFULL // 2, 0, k, width=TWIN, rows=3, last=True)
                bn_chunk(b, NFULL - 3, t0 + NFULL - 3, [k + 1])
                split_lo(t0 + NFULL, 0, TWIN)
                bn_chunk(b, NFULL - 2, t0 + NFULL - 2, [k + 2])
                bn_chunk(b, NFULL - 1, t0 + NFULL - 1, [k + 3])
                bn_chunk(b, NFULL, t0 + NFULL, [k + 4, k + 5], width=TAIL, rows=2, last=True)
                mark[0] = k + 5

                mark[0] += 1
                hold(ve, dve_step, b * PER_IMAGE + mark[0] + base[0])
                chain(V.bn_aggr(sm[:, 0:2], stats[:, :]), b)
                chain(V.tensor_copy(sm[:, 2:3], sm[:, 0:1]), b)
                chain(V.tensor_tensor(sm[:, 3:4], sm[:, 0:1], sm[:, 0:1], ALU.mult), b)
                V.tensor_tensor(sm[:, 3:4], sm[:, 3:4], sm[:, 1:2], ALU.add).then_inc(st_in, 1)
                img_rows = img[:, LEAD:LEAD + TROWS * PITCH].rearrange("p (r s) -> p r s", s=PITCH)
                chain(V.tensor_tensor(img_rows[:, :, 0], img_rows[:, :, 0], img_rows[:, :, PITCH - 1], ALU.add), b)
                chain(V.tensor_copy(img_rows[:, :, PITCH - 1], img_rows[:, :, 0]), b)
                chain(V.tensor_tensor(img_rows[:, 0, :], img_rows[:, 0, :], img_rows[:, TROWS - 1, :], ALU.add), b)
                chain(V.tensor_copy(img_rows[:, TROWS - 1, :], img_rows[:, 0, :]), b)
                ve.wait_ge(st_pe, b + 1)
                chain(V.tensor_copy(sm[:, 4:6], ps[:, 4, 0:2]), b)
                chain(V.tensor_tensor(sm[:, 6:7], sm[:, 4:5], sm[:, 4:5], ALU.mult), b)
                chain(V.scalar_tensor_tensor(sm[:, 7:8], sm[:, 5:6], GN_EPS, sm[:, 6:7], ALU.add, ALU.subtract), b)
                V.tensor_copy(cur[:, 1, 0:1], sm[:, 4:5]).then_inc(st_var, 1)
                ve.wait_ge(st_std, b + 1)
                inv, tmp, var = sm[:, 10:11], sm[:, 11:12], sm[:, 7:8]
                chain(V.reciprocal(inv, sm[:, 8:9]), b)
                chain(V.tensor_tensor(tmp, inv, inv, ALU.mult), b)
                chain(V.tensor_tensor(tmp, tmp, var, ALU.mult), b)
                chain(V.tensor_scalar(tmp, tmp, -0.5, 1.5, ALU.mult, ALU.add), b)
                chain(V.tensor_tensor(inv, inv, tmp, ALU.mult), b)
                chain(V.tensor_scalar(cur[:, 1, 1:2], inv, YS, None, ALU.mult), b)
                chain(V.tensor_scalar(cur[:, 1, 2:3], inv, var, WS, ALU.mult, ALU.mult), b)
                t1 = step(b, 1, 0)

                def y1(n, r, t, width=WIN):
                    s = slot(1, r)
                    ve.wait_ge(lo_ready, t + 1)
                    normalize(xy[:, s, 0:width], img[:, bass.ds(LEAD + n * CH, width)], 1).then_inc(y_ready, 1)

                y1(0, 0, t1)
                weights(b, 1, w132[:, :])
                per_image = mark[0]
                with ve.Fori(0, NFULL // 2 - 1) as i:
                    for r in range(2):
                        n = i * 2 + r
                        y1(n + 1, 1 - r, t1 + n + 1)
                        split_lo(t1 + n, slot(1, r))
                y1(NFULL - 1, 1, t1 + NFULL - 1)
                split_lo(t1 + NFULL - 2, slot(1, 0))
                y1(NFULL, 0, t1 + NFULL, TWIN)
                split_lo(t1 + NFULL - 1, slot(1, 1))
                split_lo(t1 + NFULL, slot(1, 0), TWIN)
            assert per_image == PER_IMAGE, (per_image, PER_IMAGE)


Z_ZPAD = 1
Z_SUMS = 2
Z_MOM = Z_SUMS + 4 + 16
Z_VAR = Z_MOM + 4
Z_WA = Z_VAR + 5 + 3 + 3
Z_FORMS = Z_WA + 1 + 6 + 1
Z_BNVAR = Z_FORMS + 2 + 2 + 3 + 2 + 3 + 2 + 2
Z_ANGLE = Z_BNVAR + 5 + 1 + 3 + 1
Z_COSARG = Z_ANGLE + 1
Z_PHASE = Z_COSARG + 2
Z_T = Z_PHASE + 10 + 6 + 18
Z_TAPS = Z_T + 1


def constants():
    import numpy as np

    k = np.zeros((P, NCONST), np.float32)

    def put(name, a):
        lo, hi = COL[name]
        a = np.asarray(a, np.float32)
        k[0:a.shape[0], lo:hi] = a.reshape(a.shape[0], hi - lo)

    p = np.arange(P)
    ch = p % C
    put("mask_g", (p[:, None] // C) == (p[None, :] // C))
    put("fold", ch[:, None] == np.arange(C)[None, :])
    put("gm", (ch[:, None] // GROUP == ch[None, :] // GROUP) * (FOUT / (GROUP * NPIX)))
    put("rep", np.arange(C)[:, None] == ch[None, :])
    c16 = np.arange(C)
    put("pair", (c16[:, None] // GROUP == c16[None, :] // GROUP) / GROUP)
    put("id16", np.eye(C))
    put("ones", np.ones((P, P)))
    half, r, ci = p // 64, p // 32 % 2, p // 16 % 2
    id0, id1 = np.zeros((P, 2, 2, 64)), np.zeros((P, 2, 2, 64))
    for kind in range(2):
        rows0 = 2 * (half if kind == 0 else 1 - half) + r
        rows1 = 2 * (half if kind == 0 else 1 - half) + 1 - r
        for dj in range(2):
            for m in range(64):
                a, e, o_ = m // 32, m // 16 % 2, m % 16
                id0[:, kind, dj, m] = (ch == o_) & (rows0 == 2 - a) & (2 * dj + ci == 2 - e)
                id1[:, kind, dj, m] = (ch == o_) & (rows1 == 1 + a) & (2 * dj + 1 - ci == 1 + e)
    put("id0", id0)
    put("id1", id1)
    put("pmask", np.stack([ci == 1, ci == 0], 1))
    put("row0", (half == 1) & (r == 0))
    put("rown", ~((half == 1) & (r == 0)))
    f = np.array([0, 1, -1])
    f1, f2, f3 = (a.ravel() for a in np.meshgrid(f, f, f, indexing="ij"))
    fs = f1 + f2 + f3
    pp, qq = np.meshgrid(np.arange(3), np.arange(3), indexing="ij")
    ang = 2 * np.pi / 3 * (f1[:, None] + f2[:, None] * pp.ravel() + f3[:, None] * qq.ravel())
    g = WS / K3
    put("u", np.concatenate([np.cos(ang), -np.sin(ang)]) * g)
    put("v", np.concatenate([np.sin(ang), np.cos(ang)]) * g)
    put("cm", np.tile(np.abs(fs)[:, None] == np.arange(4), (2, 1)))
    put("sm", np.tile((np.abs(fs)[:, None] == np.arange(1, 4)) * np.sign(fs)[:, None], (2, 1)))
    return k


def lay_out(x, wr, wi, rot_w, rot_b, gamma, beta, w1):
    import numpy as np

    x = np.asarray(x)
    x_pix = np.ascontiguousarray(x.reshape(B, C, P, PXP).transpose(0, 2, 3, 1)).reshape(B, P, PXP * C)
    t = np.zeros((B, P, FIN), np.float32)
    rows = np.zeros((B, 4, 2, C, TROWS + 1, PITCH), np.float32)
    rows[:, :, :, :, 1:TROWS, 1:] = x.reshape(B, C, H // 4, 4, W // 2, 2).transpose(0, 3, 5, 1, 2, 4)
    t[:, :, 0:FIN - 1] = rows.reshape(B, P, FIN - 1)
    wf = np.concatenate([np.asarray(a).reshape(C, C, K3).transpose(2, 1, 0).reshape(K3, C * C) for a in (wr, wi)])
    small = np.ascontiguousarray(np.broadcast_to(
        np.concatenate([np.asarray(rot_b), np.asarray(gamma), np.asarray(beta)])[None, :], (P, 9)))
    w1 = np.asarray(w1)
    band = np.zeros((2, 2, 2, C, 2, 2, 2, 2, C), np.float32)
    for half in range(2):
        for r in range(2):
            for ci in range(2):
                for kind in range(2):
                    row = 2 * (half if kind == 0 else 1 - half) + 1 - r
                    for dj in range(2):
                        col = 2 * dj + 1 - ci
                        for a in range(2):
                            for e in range(2):
                                if 0 <= row - a < 3 and 0 <= col - e < 3:
                                    band[half, r, ci, :, kind, dj, a, e, :] = w1[:, :, 2 - (row - a), 2 - (col - e)].T
    return {"x_pix": x_pix, "x_tiles": t, "wf": np.ascontiguousarray(wf),
            "rotw": np.ascontiguousarray(np.asarray(rot_w).T), "small": small, "w1band": band.reshape(P, 256),
            "consts": constants()}


def kernel(x, L0_conv_w_fft_real, L0_conv_w_fft_imag, L0_conv_rot_w, L0_conv_rot_b, L0_conv_bn_gamma,
           L0_conv_bn_beta, L1_conv_weight):
    import numpy as np
    import concourse.bacc as bacc
    from concourse.bass_utils import run_bass_kernel_spmd

    arrays = lay_out(x, L0_conv_w_fft_real, L0_conv_w_fft_imag, L0_conv_rot_w, L0_conv_rot_b,
                     L0_conv_bn_gamma, L0_conv_bn_beta, L1_conv_weight)
    nc = bacc.Bacc("TRN2", target_bir_lowering=False, num_devices=1)
    args = [nc.dram_tensor(name, a.shape, F32, kind="ExternalInput").ap() for name, a in arrays.items()]
    out = nc.dram_tensor("out", (B, P, FOUT), F32, kind="ExternalOutput").ap()
    conv_program(nc, *args, out)
    got = run_bass_kernel_spmd(nc, [arrays], core_ids=[0]).results[0]["out"]
    got = got.reshape(B, 4, 2, C, TROWS, PITCH)[..., :PITCH - 1].transpose(0, 3, 4, 1, 5, 2)
    return np.ascontiguousarray(got.reshape(B, C, 4 * TROWS, W)[:, :, 2:2 + H, :])
```

```python
from contextlib import ExitStack

import concourse.bass as bass
from concourse import mybir

F32 = mybir.dt.float32
F16 = mybir.dt.float16
ALU = mybir.AluOpType
ACT = mybir.ActivationFunctionType
AX = mybir.AxisListType

B, C, H, W = 8, 16, 512, 512
P = 128
NPIX = H * W
GROUP = 2
K3 = 27
PITCH = W // 2 + 1
TROWS = H // 4 + 1
FOUT = TROWS * PITCH
FIN = (TROWS + 1) * PITCH + 1
BANK = 512
CB = 3
CH = CB * BANK
NFULL = FOUT // CH
NCH = NFULL + 1
TAIL = FOUT - NFULL * CH
TWIN = FIN - NFULL * CH
ROWS_CH = 6
NS = 4
RING = NS * CH
STEPS = 2 * NCH
LAG = 3
BNLAG = 4
LEAD = 8
GN_EPS, BN_EPS = 1e-5, 1e-5
YS = 16.0
WS = 64.0

PXP = NPIX // P
ACHUNK = 4096
NACH = PXP * C // ACHUNK
ASLOTS = 4

_COLS = [("mask_g", 128), ("fold", 16), ("gm", 128), ("rep", 128), ("pair", 16), ("id16", 16),
         ("ones", 128), ("id0", 256), ("id1", 256), ("pmask", 2), ("row0", 1), ("rown", 1),
         ("u", 9), ("v", 9), ("cm", 4), ("sm", 3)]
COL = {}
_at = 0
for _n, _w in _COLS:
    COL[_n] = (_at, _at + _w)
    _at += _w
NCONST = _at


def conv_program(nc, x_pix, x_tiles, wf, rotw, small, w1band, consts, out):
    ctx = ExitStack()
    with ctx:
        def sb(name, shape, dt=F32):
            return ctx.enter_context(nc.sbuf_tensor(name, shape, dt))

        def sem(name):
            return ctx.enter_context(nc.semaphore(name))

        img = sb("img", [P, LEAD + FIN + 1])
        xy = sb("xy", [P, NS, CH])
        nat = sb("nat", [P, 2, RING + 2], F16)
        shf = sb("shf", [P, 2, 2, CH + 2], F16)
        wc = sb("wc", [P, 2, 2, 2, 2, 64], F16)
        cst = sb("cst", [P, NCONST])
        w32 = sb("w32", [P, 256])
        w132 = sb("w132", [P, 256])
        wtmp = sb("wtmp", [P, 256])
        stats = sb("stats", [P, (CB * NFULL + 2) * 6])
        gnp = sb("gnp", [P, 3, B])
        cur = sb("cur", [P, 2, 3])
        sm = sb("sm", [P, 32])
        smallp = sb("smallp", [P, 9])
        rw = sb("rw", [C, 3])
        wfs = sb("wfs", [2 * K3, 256])
        zc = sb("zc", [P, 320])
        zt = sb("zt", [2 * K3, 9 * B])
        zero = sb("zero", [P, 16], F16)
        zerof = sb("zerof", [P, PITCH])
        ps = ctx.enter_context(nc.psum_tensor("ps", [P, 8, 512], F32))

        taps = nc.dram_tensor("taps_scratch", [B, C, 5, 5, C], F32).ap()
        bands = nc.dram_tensor("bands_scratch", [B, P, 256], F32).ap()

        apix = img[:, 0:ASLOTS * ACHUNK].rearrange("p (s n) -> p s n", s=ASLOTS)
        o = ASLOTS * ACHUNK
        psums = img[:, o:o + B * NACH * C].rearrange("p (b j c) -> p b j c", b=B, j=NACH)
        o += B * NACH * C
        gmask = img[:, o:o + B * P].rearrange("p (b q) -> p b q", b=B)
        o += B * P
        sumc = img[:, o:o + B * C].rearrange("p (b c) -> p b c", b=B)
        o += B * C
        gram = img[0:C, o:o + B * C].rearrange("p (b c) -> p b c", b=B)
        o += B * C
        band0 = img[:, o:o + B * 256].rearrange("p (b m) -> p b m", b=B)
        o += B * 256
        tapsb = img[0:9 * B, o:o + 256]
        o += 256
        zpad = img[:, o:o + 400]

        def c(name, parts=P):
            a, z = COL[name]
            return cst[0:parts, a:z]

        const_in = sem("const_in")
        primed = sem("primed")
        a_in = [sem(f"a_in{s}") for s in range(ASLOTS)]
        a_gram = sem("a_gram")
        a_sum = sem("a_sum")
        a_zero = sem("a_zero")
        a_mask = sem("a_mask")
        zpe = sem("zpe")
        zve = sem("zve")
        zac = sem("zac")
        zdma = sem("zdma")
        dve_step = sem("dve_step")
        x_in = [sem(f"x_in{s}") for s in range(NS)]
        w_in = sem("w_in")
        y_ready = sem("y_ready")
        hi_ready = sem("hi_ready")
        lo_ready = sem("lo_ready")
        shf_in = [sem(f"shf_in{s}") for s in range(2)]
        w_ready = sem("w_ready")
        pe_done = sem("pe_done")
        evac_done = sem("evac_done")
        st_in = sem("st_in")
        st_pe = sem("st_pe")
        st_var = sem("st_var")
        st_std = sem("st_std")
        out_done = [sem(f"out_done{s}") for s in range(2)]

        y_raw = sem("y_raw")
        lo_part = sem("lo_part")
        row_done = sem("row_done")
        col_done = sem("col_done")
        passed = sem("passed")

        def hold(eng, signal, value):
            eng.wait_ge(signal, value)
            eng.sem_inc(passed, 1)

        block = ctx.enter_context(nc.Block())

        def step(b, layer, n):
            return b * STEPS + layer * NCH + n

        def ring(layer, r):
            return (layer * NCH + r) % NS

        def shf_count(b, layer, i, r):
            s = ring(layer, r)
            rounds = b * (STEPS // NS) + (layer * NCH) // NS + i + ((layer * NCH) % NS + r) // NS
            return rounds * (64 if s % 2 == 0 else 80) + (32, 32, 64, 80)[s]

        HALF = NCH // 2

        @block.sync
        def _(sp):
            for dst, src in ((cst[:, :], consts), (rw[:, :], rotw), (smallp[:, :], small),
                             (wfs[:, :], wf), (w132[:, :], w1band)):
                sp.dma_start(dst, src).then_inc(const_in, 16)
            with sp.Fori(0, B) as b:
                with sp.Fori(0, NACH // ASLOTS) as jj:
                    for s in range(ASLOTS):
                        k = b * NACH + jj * ASLOTS + s
                        hold(sp, a_gram, k + 1)
                        hold(sp, a_sum, k + 1)
                        sp.dma_start(apix[:, s, :], x_pix[b, :, bass.ds((jj * ASLOTS + s) * ACHUNK, ACHUNK)]
                                     ).then_inc(a_in[s], 16)
            hold(sp, zve, Z_ZPAD)
            sp.dma_start(taps.rearrange("b c p q o -> (b c) (p q o)"), zpad).then_inc(zdma, 16)
            hold(sp, zdma, 16)
            hold(sp, zve, Z_TAPS)
            for t in range(9):
                sp.dma_start(taps[:, :, 1 + t // 3, 1 + t % 3, :],
                             tapsb[t * B:(t + 1) * B, :].rearrange("p (c o) -> p c o", c=C)).then_inc(zdma, 16)
            hold(sp, zdma, 16 * 10)
            n = 10
            for half in range(2):
                for r in range(2):
                    for ci in range(2):
                        g = ((half * 2 + r) * 2 + ci) * C
                        for kind in range(2):
                            row = 2 * (half if kind == 0 else 1 - half) + r
                            for dj in range(2):
                                cc = 2 * dj + ci
                                for a in range(2):
                                    m = ((kind * 2 + dj) * 2 + a) * 32
                                    src = taps[:, :, row + a, cc:cc + 2, :].rearrange("b c q o -> c b (q o)")
                                    sp.dma_start(band0[g:g + C, :, m:m + 32], src).then_inc(zdma, 16)
                                    n += 1
            hold(sp, zdma, 16 * n)
            sp.dma_start(bands.rearrange("b p m -> p b m"), band0).then_inc(zdma, 16)
            hold(sp, zdma, 16 * (n + 1))

            def load_x(b, i, r, width=CH):
                n = i * NS + r
                hold(sp, lo_ready, step(b, 0, n) + 1)
                sp.dma_start(xy[:, r, 0:width], x_tiles[b, :, bass.ds(n * CH, width)]).then_inc(x_in[r], 16)

            def make_shifted(t, layer, r, last=False):
                hold(sp, lo_ready, t + (5 if last else 6))
                hold(sp, pe_done, t + 3)
                s = ring(layer, r)
                q, base, width = s % 2, s * CH, (TAIL if last else CH) + 1
                sp.dma_start(shf[64:128, q, :, 0:width], nat[64:128, :, base:base + width]).then_inc(shf_in[q], 16)
                cuts = [0, width] if s < NS - 1 else [0, min(CH - PITCH, width // 2 if last else CH), width]
                for a, z in zip(cuts[:-1], cuts[1:]):
                    src = (base + PITCH + a) % RING
                    sp.dma_start(shf[0:64, q, :, a:z], nat[0:64, :, src:src + z - a]).then_inc(shf_in[q], 16)

            def store(b, i, r, width=CH):
                n = i * 2 + r
                hold(sp, evac_done, step(b, 1, n) + 9)
                hold(sp, out_done[r], 16 * (b * HALF + i + HALF))
                sp.dma_start(out[b, :, bass.ds(n * CH, width)], img[:, bass.ds(LEAD + n * CH, width)]
                             ).then_inc(out_done[r], 16)

            def store_late(b, k):
                n = NCH - 4 + k
                store(b, n // 2, n % 2, TAIL if n == NFULL else CH)

            with sp.Fori(0, B) as b:
                t0 = step(b, 0, 0)
                for n in range(NS):
                    load_x(b, 0, n)
                hold(sp, w_ready, 2 * b + 1)
                sp.dma_start(w32[:, :], bands[b]).then_inc(w_in, 16)
                for n in range(NS):
                    load_x(b, 1, n)
                    with sp.If(b > 0):
                        store_late(nc.s_assert_within(b - 1, 0, B - 1, skip_runtime_bounds_check_because="b > 0 here"), n)
                    make_shifted(t0 + n, 0, n)
                with sp.Fori(1, 4) as i:
                    for r in range(NS):
                        load_x(b, i + 1, r)
                        make_shifted(t0 + i * NS + r, 0, r)
                load_x(b, 5, 0)
                make_shifted(t0 + 16, 0, 0)
                load_x(b, 5, 1, TWIN)
                for n in range(17, NCH):
                    make_shifted(t0 + n, 0, n % NS, last=(n == NFULL))
                t1 = step(b, 1, 0)
                for n in range(NS):
                    make_shifted(t1 + n, 1, n)
                with sp.Fori(1, 5) as i:
                    for r in range(NS):
                        make_shifted(t1 + i * NS + r, 1, r)
                        store(b, i * 2 + r // 2 - 2, r % 2)
                make_shifted(t1 + 20, 1, 0)
                store(b, 8, 0)
                make_shifted(t1 + 21, 1, 1, last=True)
                store(b, 8, 1)
            for k in range(4):
                store_late(B - 1, k)
            for r in range(2):
                sp.wait_ge(out_done[r], 16 * (B + 1) * HALF)

        @block.tensor
        def _(pe):
            pe.sem_inc(a_gram, ASLOTS)
            pe.sem_inc(pe_done, 4)
            pe.wait_ge(a_zero, 1)
            with pe.Fori(0, B // 2) as bb:
                for h in range(2):
                    b = bb * 2 + h
                    acc = ps[:, h, 0:P]
                    pe.wait_ge(a_mask, b + 1)
                    nc.tensor.matmul(acc, zerof[:, 0:P], zerof[:, 0:P], start=True, stop=False)
                    with pe.Fori(0, NACH // ASLOTS) as jj:
                        for s in range(ASLOTS):
                            pe.wait_ge(a_in[s], 16 * (b * (NACH // ASLOTS) + jj + 1))
                            for q in range(ACHUNK // P):
                                blk = apix[:, s, q * P:(q + 1) * P]
                                mm = nc.tensor.matmul(acc, blk, blk, start=False, stop=False)
                            mm.then_inc(a_gram, 1)
                    nc.tensor.matmul(acc, zerof[:, 0:P], zerof[:, 0:P], start=False, stop=True).then_inc(zpe, 1)
            done = B

            def mm(out_, lhs, rhs, last=True):
                m = nc.tensor.matmul(out_, lhs, rhs, start=True, stop=True)
                if last:
                    m.then_inc(zpe, 1)

            pe.wait_ge(const_in, 16 * 5)
            pe.wait_ge(zve, Z_SUMS)
            for h in range(2):
                mm(ps[0:C, 2 + h, 0:512], c("fold"), gmask[:, 4 * h:4 * h + 4, :].rearrange("p b q -> p (b q)"), False)
            for b in range(B):
                mm(ps[0:C, 4, b:b + 1], sumc[:, b, :], c("ones")[:, 0:1], b == B - 1)
            pe.wait_ge(zve, Z_MOM)
            mm(ps[0:C, 4, 16:32], c("pair", C), zc[0:C, 0:16])
            pe.wait_ge(zve, Z_WA)
            for b in range(B):
                mm(ps[0:C, 4, 64 + 3 * b:67 + 3 * b], gram[:, b, :], zc[0:C, 72 + 3 * b:75 + 3 * b], b == B - 1)
            pe.wait_ge(zve, Z_FORMS)
            mm(ps[:, 5, 0:72], c("ones", C), zc[0:C, 96:168], False)
            mm(ps[:, 5, 128:152], c("rep", C), zc[0:C, 40:64])
            pe.wait_ge(zve, Z_T)
            mm(ps[0:9 * B, 6, 0:256], zt[:, :], wfs[:, :])


            def chunk(b, layer, i, r, width=CH, last=False):
                n = i * NS + r
                t = step(b, layer, n)
                s = ring(layer, r)
                pe.wait_ge(lo_ready, t + (5 if last else 6))
                pe.wait_ge(evac_done, t + 7)
                pe.wait_ge(shf_in[s % 2], shf_count(b, layer, i, r))
                for q in range((width + BANK - 1) // BANK):
                    w = min(BANK, width - q * BANK)
                    k = 0
                    for whl, xhl in ((0, 0), (1, 0), (0, 1)):
                        for dj in range(2):
                            for kind in range(2):
                                at_ = q * BANK + dj
                                tiles = shf[:, s % 2, xhl, at_:at_ + w] if kind else \
                                    nat[:, xhl, s * CH + at_:s * CH + at_ + w]
                                done = nc.tensor.matmul(
                                    ps[64 * kind:64 * kind + 64, CB * (s % 2) + q, 0:w],
                                    wc[:, layer, whl, kind, dj, :], tiles, start=(k == 0), stop=(k == 5))
                            k += 1
                done.then_inc(pe_done, 1)

            with pe.Fori(0, B) as b:
                for layer in range(2):
                    if layer == 1:
                        pe.wait_ge(st_in, b + 1)
                        nc.tensor.matmul(ps[:, 6, 0:2], c("gm"), sm[:, 2:4], start=True, stop=True).then_inc(st_pe, 1)
                    hold(pe, w_ready, 2 * b + layer + 2)
                    with pe.Fori(0, 5) as i:
                        for r in range(NS):
                            chunk(b, layer, i, r)
                    chunk(b, layer, 5, 0)
                    chunk(b, layer, 5, 1, TAIL, last=True)

        @block.scalar
        def _(act):
            act.sem_inc(evac_done, 8)
            act.wait_ge(zve, Z_VAR)
            nc.scalar.activation(zc[0:C, 64:72], zc[0:C, 32:40], ACT.Sqrt).then_inc(zac, 1)
            act.wait_ge(zve, Z_BNVAR)
            nc.scalar.activation(zc[:, 176:179], zc[:, 172:175], ACT.Sqrt).then_inc(zac, 1)
            act.wait_ge(zve, Z_ANGLE)
            nc.scalar.activation(zc[:, 232:240], zc[:, 224:232], ACT.Tanh).then_inc(zac, 1)
            act.wait_ge(zve, Z_COSARG)
            nc.scalar.activation(zc[:, 248:256], zc[:, 240:248], ACT.Sin).then_inc(zac, 1)
            act.wait_ge(zve, Z_PHASE)
            nc.scalar.activation(zc[:, 272:288], zc[:, 256:272], ACT.Sin).then_inc(zac, 1)


            def round_hi(b, layer, i, r, width=CH):
                t = step(b, layer, i * NS + r)
                s = ring(layer, r)
                act.wait_ge(y_ready, t + 1)
                act.wait_ge(pe_done, t + 1)
                nc.scalar.activation(nat[:, 0, s * CH:s * CH + width], xy[:, s, 0:width], ACT.Identity
                                     ).then_inc(hi_ready, 1)

            def evacuate(b, layer, i, r, width=CH):
                n = i * 2 + r
                t = step(b, layer, n)
                if layer == 0:
                    act.wait_ge(out_done[r], 16 * (b * HALF + i + 1))
                act.wait_ge(pe_done, t + 5)
                banks = ps[:, CB * r:CB * r + CB, :].rearrange("p a b -> p (a b)")
                nc.scalar.activation(img[:, bass.ds(LEAD + n * CH, width)], banks[:, 0:width], ACT.Identity,
                                     bias=cur[:, layer, 0:1], scale=1.0 / (YS * WS)).then_inc(evac_done, 1)

            def evacuate_n(b, layer, n):
                evacuate(b, layer, n // 2, n % 2, TAIL if n == NFULL else CH)

            with act.Fori(0, B) as b:
                for layer in range(2):
                    for n in range(NS):
                        round_hi(b, layer, 0, n)
                        if n >= LAG:
                            evacuate_n(b, layer, n - LAG)
                        elif layer == 0:
                            with act.If(b > 0):
                                evacuate_n(nc.s_assert_within(b - 1, 0, B - 1, skip_runtime_bounds_check_because="b > 0 here"),
                                           1, NCH - LAG + n)
                    with act.Fori(1, 5) as i:
                        for r in range(NS):
                            round_hi(b, layer, i, r)
                            evacuate(b, layer, i * 2 + (r + 1) // 2 - 2, (r + 1) % 2)
                    for n in (20, 21):
                        round_hi(b, layer, 5, n % NS, TWIN if n == NFULL else CH)
                        evacuate_n(b, layer, n - LAG)
                    if layer == 0:
                        for n in range(NCH - LAG, NCH):
                            evacuate_n(b, 0, n)
                        act.wait_ge(st_var, b + 1)
                        nc.scalar.activation(sm[:, 8:9], sm[:, 7:8], ACT.Sqrt).then_inc(st_std, 1)
            for n in range(NCH - LAG, NCH):
                evacuate_n(B - 1, 1, n)

        @block.vector
        def _(ve):
            V = nc.vector
            ve.sem_inc(a_sum, ASLOTS)
            ve.sem_inc(a_mask, 2)
            ve.sem_inc(lo_ready, 4)
            ve.sem_inc(w_ready, 1)
            ve.sem_inc(out_done[0], 16 * HALF)
            ve.sem_inc(out_done[1], 16 * HALF)
            V.memset(zero[:, :], 0.0)
            V.memset(zerof[:, :], 0.0).then_inc(a_zero, 1)
            V.memset(img[:, LEAD + FOUT:], 0.0).then_inc(dve_step, 1)
            ve.wait_ge(const_in, 16 * 5)
            with ve.Fori(0, B // 2) as bb:
                for h in range(2):
                    b = bb * 2 + h
                    with ve.Fori(0, NACH // ASLOTS) as jj:
                        for s in range(ASLOTS):
                            ve.wait_ge(a_in[s], 16 * (b * (NACH // ASLOTS) + jj + 1))
                            V.tensor_reduce(psums[:, b, bass.ds(jj * ASLOTS + s, 1), :].rearrange("p j c -> p (j c)"),
                                            apix[:, s, :].rearrange("p (k c) -> p c k", c=C),
                                            AX.X, ALU.add).then_inc(a_sum, 1)
                    ve.wait_ge(zpe, b + 1)
                    V.tensor_tensor(gmask[:, bass.ds(b, 1), :].rearrange("p b q -> p (b q)"), ps[:, h, 0:P],
                                    c("mask_g"), ALU.mult).then_inc(a_mask, 1)

            count = [0]

            def link(ins):
                count[0] += 1
                ins.then_inc(zve, 1)
                ve.wait_ge(zve, count[0])
                return count[0]

            pe_steps = [B]
            act_steps = [0]

            def after_pe():
                pe_steps[0] += 1
                ve.wait_ge(zpe, pe_steps[0])

            def after_act():
                act_steps[0] += 1
                ve.wait_ge(zac, act_steps[0])

            def at(k, n):
                assert k == n, (k, n)

            at(link(V.memset(zpad, 0.0)), Z_ZPAD)
            ve.wait_ge(a_mask, B + 2)
            ve.wait_ge(a_sum, B * NACH + ASLOTS)
            at(link(V.tensor_reduce(sumc, psums.rearrange("p b j c -> p b c j"), AX.X, ALU.add)), Z_SUMS)
            after_pe()
            for hh in range(2):
                link(V.tensor_reduce(gram[:, 4 * hh:4 * hh + 4, :],
                                     ps[0:C, 2 + hh, :].rearrange("p (b k c) -> p b c k", b=4, k=8),
                                     AX.X, ALU.add))
            link(V.tensor_scalar(gram, gram, 1.0 / NPIX, None, ALU.mult))
            link(V.tensor_scalar(zc[0:C, 0:8], ps[0:C, 4, 0:8], 1.0 / NPIX, None, ALU.mult))
            for b in range(B):
                link(V.tensor_tensor(zc[0:C, 296:312], gram[:, b, :], c("id16", C), ALU.mult))
                n = link(V.tensor_reduce(zc[0:C, 8 + b:9 + b], zc[0:C, 296:312], AX.X, ALU.add))
            at(n, Z_MOM)
            after_pe()
            gmean, var, std, inv = zc[0:C, 40:48], zc[0:C, 32:40], zc[0:C, 64:72], zc[0:C, 16:24]
            tmp = zc[0:C, 24:32]
            link(V.tensor_copy(gmean, ps[0:C, 4, 16:24]))
            link(V.tensor_tensor(tmp, gmean, gmean, ALU.mult))
            link(V.tensor_tensor(var, ps[0:C, 4, 24:32], tmp, ALU.subtract))
            at(link(V.tensor_scalar(var, var, GN_EPS, None, ALU.add)), Z_VAR)

            def newton(inv, std, var, tmp):
                link(V.reciprocal(inv, std))
                link(V.tensor_tensor(tmp, inv, inv, ALU.mult))
                link(V.tensor_tensor(tmp, tmp, var, ALU.mult))
                link(V.tensor_scalar(tmp, tmp, -0.5, 1.5, ALU.mult, ALU.add))
                link(V.tensor_tensor(inv, inv, tmp, ALU.mult))

            after_act()
            newton(inv, std, var, tmp)
            link(V.tensor_scalar(zc[0:C, 48:56], inv, YS, None, ALU.mult))
            link(V.tensor_tensor(tmp, inv, var, ALU.mult))
            link(V.tensor_scalar(zc[0:C, 56:64], tmp, WS, None, ALU.mult))
            wa = zc[0:C, 72:96].rearrange("p (b o) -> p b o", o=3)
            for k in range(3):
                n = link(V.tensor_scalar(wa[:, :, k], inv, rw[:, k:k + 1], None, ALU.mult))
            at(n, Z_WA)
            forms = zc[0:C, 96:168].rearrange("p (f b o) -> p f b o", f=3, o=3)
            link(V.tensor_tensor(tmp, zc[0:C, 0:8], gmean, ALU.subtract))
            for k in range(3):
                link(V.tensor_tensor(forms[:, 1, :, k], wa[:, :, k], zc[0:C, 0:8], ALU.mult))
                link(V.tensor_tensor(forms[:, 2, :, k], wa[:, :, k], tmp, ALU.mult))
            after_pe()
            at(link(V.tensor_tensor(zc[0:C, 96:120], zc[0:C, 72:96], ps[0:C, 4, 64:88], ALU.mult)), Z_FORMS)
            after_pe()
            q = zc[:, 96:168]
            link(V.tensor_copy(q, ps[:, 5, 0:72]))
            link(V.tensor_copy(gnp[:, :, :], ps[:, 5, 128:152].rearrange("p (f b) -> p f b", f=3)))
            qz, qm, qs = q[:, 0:24], q[:, 24:48], q[:, 48:72]

            def bo(a):
                return a.rearrange("p (b o) -> p b o", o=3)

            def ob(a):
                return a.rearrange("p (b o) -> p o b", o=3)

            link(V.tensor_tensor(qm, qm, qm, ALU.mult))
            link(V.tensor_tensor(qz, qz, qm, ALU.subtract))
            for k in range(3):
                link(V.tensor_scalar(bo(qs)[:, :, k], bo(qs)[:, :, k], smallp[:, k:k + 1], None, ALU.add))
            zm = zc[:, 168:171]
            link(V.tensor_reduce(zm, ob(qs), AX.X, ALU.add))
            link(V.tensor_scalar(zm, zm, 1.0 / B, None, ALU.mult))
            for k in range(3):
                link(V.tensor_scalar(bo(qs)[:, :, k], bo(qs)[:, :, k], zm[:, k:k + 1], None, ALU.subtract))
            link(V.tensor_tensor(qm, qs, qs, ALU.mult))
            link(V.tensor_tensor(qz, qz, qm, ALU.add))
            bv = zc[:, 172:175]
            link(V.tensor_reduce(bv, ob(qz), AX.X, ALU.add))
            at(link(V.tensor_scalar(bv, bv, 1.0 / B, BN_EPS, ALU.mult, ALU.add)), Z_BNVAR)
            after_act()
            bi = zc[:, 180:183]
            newton(bi, zc[:, 176:179], bv, zc[:, 184:187])
            link(V.tensor_tensor(bi, bi, smallp[:, 3:6], ALU.mult))
            for k in range(3):
                link(V.tensor_scalar(bo(qs)[:, :, k], bo(qs)[:, :, k], bi[:, k:k + 1], smallp[:, 6 + k:7 + k],
                                     ALU.mult, ALU.add))
            at(link(V.tensor_reduce(zc[:, 224:232], bo(qs), AX.X, ALU.add)), Z_ANGLE)
            after_act()
            pi = 3.141592653589793
            at(link(V.tensor_scalar(zc[:, 240:248], zc[:, 232:240], pi / 4, pi / 2, ALU.mult, ALU.add)), Z_COSARG)
            after_act()
            link(V.tensor_scalar(zc[:, 256:264], zc[:, 248:256], 2 * pi / 3, None, ALU.mult))
            at(link(V.tensor_scalar(zc[:, 264:272], zc[:, 248:256], -2 * pi / 3, pi / 2, ALU.mult, ALU.add)), Z_PHASE)
            after_act()
            s1, c1 = zc[:, 272:280], zc[:, 280:288]
            s2, c2, s3, c3 = zc[:, 192:200], zc[:, 200:208], zc[:, 208:216], zc[:, 216:224]
            t8 = zc[:, 288:296]
            link(V.tensor_tensor(s2, s1, c1, ALU.mult))
            link(V.tensor_scalar(s2, s2, 2.0, None, ALU.mult))
            link(V.tensor_tensor(c2, c1, c1, ALU.mult))
            link(V.tensor_scalar(c2, c2, 2.0, -1.0, ALU.mult, ALU.add))
            link(V.tensor_tensor(s3, s2, c1, ALU.mult))
            link(V.tensor_tensor(t8, c2, s1, ALU.mult))
            link(V.tensor_tensor(s3, s3, t8, ALU.add))
            link(V.tensor_tensor(c3, c2, c1, ALU.mult))
            link(V.tensor_tensor(t8, s2, s1, ALU.mult))
            link(V.tensor_tensor(c3, c3, t8, ALU.subtract))
            n2 = 2 * K3
            cf, sf = zc[0:n2, 96:104], zc[0:n2, 104:112]
            cm, smk = c("cm", n2), c("sm", n2)
            link(V.tensor_scalar(cf, c1[0:n2, :], cm[:, 1:2], cm[:, 0:1], ALU.mult, ALU.add))
            link(V.scalar_tensor_tensor(cf, c2[0:n2, :], cm[:, 2:3], cf, ALU.mult, ALU.add))
            link(V.scalar_tensor_tensor(cf, c3[0:n2, :], cm[:, 3:4], cf, ALU.mult, ALU.add))
            link(V.tensor_scalar(sf, s1[0:n2, :], smk[:, 0:1], None, ALU.mult))
            link(V.scalar_tensor_tensor(sf, s2[0:n2, :], smk[:, 1:2], sf, ALU.mult, ALU.add))
            link(V.scalar_tensor_tensor(sf, s3[0:n2, :], smk[:, 2:3], sf, ALU.mult, ALU.add))
            for k in range(9):
                link(V.tensor_scalar(zt[:, 8 * k:8 * k + 8], cf, c("u", n2)[:, k:k + 1], None, ALU.mult))
                n = link(V.scalar_tensor_tensor(zt[:, 8 * k:8 * k + 8], sf, c("v", n2)[:, k:k + 1],
                                                zt[:, 8 * k:8 * k + 8], ALU.mult, ALU.add))
            at(n, Z_T)
            after_pe()
            at(link(V.tensor_copy(tapsb, ps[0:9 * B, 6, 0:256])), Z_TAPS)
            V.tensor_scalar(w132[:, :], w132[:, :], WS, None, ALU.mult).then_inc(dve_step, 1)
            ve.wait_ge(dve_step, 2)


            PER_IMAGE = 1 + 2 + 2 + 4 + 2 + 7 + 2
            mark = [0]

            def chain(ins, b):
                mark[0] += 1
                ins.then_inc(dve_step, 1)
                ve.wait_ge(dve_step, b * PER_IMAGE + mark[0] + 2)

            def weights(b, layer, w):
                chain(V.scalar_tensor_tensor(wtmp[:, :], c("id0" if layer == 0 else "id1"), cur[:, layer, 2:3], w,
                                             ALU.mult, ALU.add), b)
                hi = wc[:, layer, 0].rearrange("p a b m -> p (a b m)")
                lo = wc[:, layer, 1].rearrange("p a b m -> p (a b m)")
                chain(V.tensor_copy(hi, wtmp[:, :]), b)
                V.tensor_tensor(lo, wtmp[:, :], hi, ALU.subtract).then_inc(w_ready, 1)

            def normalize(dst, src, layer):
                return V.tensor_scalar(dst, src, cur[:, layer, 0:1], cur[:, layer, 1:2], ALU.subtract, ALU.mult)

            def split_lo(b, layer, i, r, width=CH):
                t = step(b, layer, i * NS + r)
                s = ring(layer, r)
                ve.wait_ge(hi_ready, t + 1)
                lo = V.tensor_tensor(nat[:, 1, s * CH:s * CH + width], xy[:, s, 0:width],
                                     nat[:, 0, s * CH:s * CH + width], ALU.subtract)
                if s == 0:
                    lo.then_inc(lo_part, 1)
                    ve.wait_ge(lo_part, b * 11 + layer * 6 + i + 1)
                    V.tensor_copy(nat[:, :, RING:RING + 1], nat[:, :, 0:1]).then_inc(lo_ready, 1)
                else:
                    lo.then_inc(lo_ready, 1)

            def y0(b, i, r, first=False, last=False):
                n = i * NS + r
                width, rows = (TWIN, 5) if last else (CH, ROWS_CH)
                ve.wait_ge(x_in[r], 16 * (b * (6 if r < 2 else 5) + i + 1))
                normalize(xy[:, r, 0:width], xy[:, r, 0:width], 0).then_inc(y_raw, 1)
                ve.wait_ge(y_raw, b * NCH + n + 1)
                if first:
                    V.tensor_copy(xy[:, r, 1:PITCH], zerof[:, 1:PITCH])
                if last:
                    V.tensor_copy(xy[:, r, TAIL + 1:TAIL + PITCH], zerof[:, 1:PITCH])
                edge = xy[:, r, bass.ds(n * (ROWS_CH * PITCH - CH), (rows - 1) * PITCH + 1)]
                V.tensor_copy(edge[:, 0:(rows - 1) * PITCH + 1:PITCH], zero[:, 0:rows]).then_inc(y_ready, 1)

            def mask_row(b, first):
                at_ = LEAD + (0 if first else FOUT - PITCH)
                V.tensor_scalar(img[:, at_:at_ + PITCH], img[:, at_:at_ + PITCH],
                                c("row0" if first else "rown"), None, ALU.mult).then_inc(row_done, 1)
                hold(ve, row_done, 2 * b + (1 if first else 2))

            def sum_x1(b, n, last=False):
                width, rows = (TAIL, 4) if last else (CH, ROWS_CH)
                ve.wait_ge(evac_done, step(b, 0, n) + 9)
                if last:
                    mask_row(b, False)
                pairs = img[:, bass.ds(LEAD - 1 + n * (ROWS_CH * PITCH), rows * PITCH)].rearrange(
                    "p (k s) -> p k s", s=PITCH)[:, :, 0:2]
                V.tensor_tensor(pairs, pairs, c("pmask").unsqueeze(1).to_broadcast([P, rows, 2]),
                                ALU.mult).then_inc(col_done, 1)
                ve.wait_ge(col_done, b * NCH + n + 1)
                for k in range((width + BANK - 1) // BANK):
                    w = min(BANK, width - BANK * k)
                    ins = V.bn_stats(stats[:, bass.ds((n * CB + k) * 6, 6)],
                                     img[:, bass.ds(LEAD + n * CH + BANK * k, w)])
                return ins

            def y1(b, i, r, width=CH):
                n = i * NS + r
                s = ring(1, r)
                ve.wait_ge(lo_ready, step(b, 1, n) + 1)
                normalize(xy[:, s, 0:width], img[:, bass.ds(LEAD + n * CH, width)], 1).then_inc(y_ready, 1)

            with ve.Fori(0, B) as b:
                mark[0] = 0
                chain(V.tensor_copy(cur[:, 0, :], gnp[:, :, bass.ds(b, 1)].rearrange("p f b -> p (f b)")), b)
                y0(b, 0, 0, first=True)
                y0(b, 0, 1)
                split_lo(b, 0, 0, 0)
                ve.wait_ge(w_in, 16 * (b + 1))
                weights(b, 0, w32[:, :])
                split_lo(b, 0, 0, 1)
                for n in (2, 3):
                    y0(b, 0, n)
                    split_lo(b, 0, 0, n)
                ve.wait_ge(evac_done, step(b, 0, 0) + 9)
                mask_row(b, True)
                with ve.Fori(1, 5) as i:
                    for r in range(NS):
                        y0(b, i, r)
                        sum_x1(b, (i - 1) * NS + r)
                        split_lo(b, 0, i, r)
                y0(b, 5, 0)
                sum_x1(b, 16)
                split_lo(b, 0, 5, 0)
                y0(b, 5, 1, last=True)
                sum_x1(b, 17)
                split_lo(b, 0, 5, 1, TWIN)
                for n in range(18, NFULL):
                    sum_x1(b, n)
                mark[0] += 1
                sum_x1(b, NFULL, last=True).then_inc(dve_step, 1)

                hold(ve, dve_step, b * PER_IMAGE + mark[0] + 2)
                chain(V.bn_aggr(sm[:, 2:4], stats[:, :]), b)
                V.scalar_tensor_tensor(sm[:, 3:4], sm[:, 2:3], sm[:, 2:3], sm[:, 3:4], ALU.mult, ALU.add
                                       ).then_inc(st_in, 1)
                img_rows = img[:, LEAD:LEAD + TROWS * PITCH].rearrange("p (r s) -> p r s", s=PITCH)
                chain(V.tensor_tensor(img_rows[:, :, 0], img_rows[:, :, 0], img_rows[:, :, PITCH - 1], ALU.add), b)
                chain(V.tensor_copy(img_rows[:, :, PITCH - 1], img_rows[:, :, 0]), b)
                chain(V.tensor_tensor(img_rows[:, 0, :], img_rows[:, 0, :], img_rows[:, TROWS - 1, :], ALU.add), b)
                chain(V.tensor_copy(img_rows[:, TROWS - 1, :], img_rows[:, 0, :]), b)
                ve.wait_ge(st_pe, b + 1)
                chain(V.tensor_copy(cur[:, 1, 0:1], ps[:, 6, 0:1]), b)
                mean = cur[:, 1, 0:1]
                chain(V.scalar_tensor_tensor(sm[:, 6:7], mean, mean, ps[:, 6, 1:2], ALU.mult, ALU.subtract), b)
                inv, tmp, var = sm[:, 10:11], sm[:, 11:12], sm[:, 7:8]
                V.tensor_scalar(var, sm[:, 6:7], -1.0, GN_EPS, ALU.mult, ALU.add).then_inc(st_var, 1)
                ve.wait_ge(st_std, b + 1)
                chain(V.reciprocal(inv, sm[:, 8:9]), b)
                chain(V.tensor_tensor(tmp, inv, inv, ALU.mult), b)
                chain(V.tensor_tensor(tmp, tmp, var, ALU.mult), b)
                chain(V.tensor_scalar(tmp, tmp, -0.5, 1.5, ALU.mult, ALU.add), b)
                chain(V.tensor_tensor(inv, inv, tmp, ALU.mult), b)
                chain(V.tensor_scalar(cur[:, 1, 1:2], inv, YS, None, ALU.mult), b)
                chain(V.tensor_scalar(cur[:, 1, 2:3], inv, var, WS, ALU.mult, ALU.mult), b)
                y1(b, 0, 0)
                y1(b, 0, 1)
                split_lo(b, 1, 0, 0)
                weights(b, 1, w132[:, :])
                per_image = mark[0]
                for n in range(1, 3):
                    y1(b, 0, n + 1)
                    split_lo(b, 1, 0, n)
                y1(b, 1, 0)
                split_lo(b, 1, 0, 3)
                with ve.Fori(1, 5) as i:
                    for r in range(NS):
                        y1(b, i + (r + 1) // NS, (r + 1) % NS)
                        split_lo(b, 1, i, r)
                y1(b, 5, 1, TWIN)
                split_lo(b, 1, 5, 0)
                split_lo(b, 1, 5, 1, TWIN)
            assert per_image == PER_IMAGE, (per_image, PER_IMAGE)


Z_ZPAD = 1
Z_SUMS = 2
Z_MOM = Z_SUMS + 4 + 16
Z_VAR = Z_MOM + 4
Z_WA = Z_VAR + 5 + 3 + 3
Z_FORMS = Z_WA + 1 + 6 + 1
Z_BNVAR = Z_FORMS + 2 + 2 + 3 + 2 + 3 + 2 + 2
Z_ANGLE = Z_BNVAR + 5 + 1 + 3 + 1
Z_COSARG = Z_ANGLE + 1
Z_PHASE = Z_COSARG + 2
Z_T = Z_PHASE + 10 + 6 + 18
Z_TAPS = Z_T + 1


def constants():
    import numpy as np

    k = np.zeros((P, NCONST), np.float32)

    def put(name, a):
        lo, hi = COL[name]
        a = np.asarray(a, np.float32)
        k[0:a.shape[0], lo:hi] = a.reshape(a.shape[0], hi - lo)

    p = np.arange(P)
    ch = p % C
    put("mask_g", (p[:, None] // C) == (p[None, :] // C))
    put("fold", ch[:, None] == np.arange(C)[None, :])
    put("gm", (ch[:, None] // GROUP == ch[None, :] // GROUP) * (FOUT / (GROUP * NPIX)))
    put("rep", np.arange(C)[:, None] == ch[None, :])
    c16 = np.arange(C)
    put("pair", (c16[:, None] // GROUP == c16[None, :] // GROUP) / GROUP)
    put("id16", np.eye(C))
    put("ones", np.ones((P, P)))
    half, r, ci = p // 64, p // 32 % 2, p // 16 % 2
    id0, id1 = np.zeros((P, 2, 2, 64)), np.zeros((P, 2, 2, 64))
    for kind in range(2):
        rows0 = 2 * (half if kind == 0 else 1 - half) + r
        rows1 = 2 * (half if kind == 0 else 1 - half) + 1 - r
        for dj in range(2):
            for m in range(64):
                a, e, o_ = m // 32, m // 16 % 2, m % 16
                id0[:, kind, dj, m] = (ch == o_) & (rows0 == 2 - a) & (2 * dj + ci == 2 - e)
                id1[:, kind, dj, m] = (ch == o_) & (rows1 == 1 + a) & (2 * dj + 1 - ci == 1 + e)
    put("id0", id0)
    put("id1", id1)
    put("pmask", np.stack([ci == 1, ci == 0], 1))
    put("row0", (half == 1) & (r == 0))
    put("rown", ~((half == 1) & (r == 0)))
    f = np.array([0, 1, -1])
    f1, f2, f3 = (a.ravel() for a in np.meshgrid(f, f, f, indexing="ij"))
    fs = f1 + f2 + f3
    pp, qq = np.meshgrid(np.arange(3), np.arange(3), indexing="ij")
    ang = 2 * np.pi / 3 * (f1[:, None] + f2[:, None] * pp.ravel() + f3[:, None] * qq.ravel())
    g = WS / K3
    put("u", np.concatenate([np.cos(ang), -np.sin(ang)]) * g)
    put("v", np.concatenate([np.sin(ang), np.cos(ang)]) * g)
    put("cm", np.tile(np.abs(fs)[:, None] == np.arange(4), (2, 1)))
    put("sm", np.tile((np.abs(fs)[:, None] == np.arange(1, 4)) * np.sign(fs)[:, None], (2, 1)))
    return k


def lay_out(x, wr, wi, rot_w, rot_b, gamma, beta, w1):
    import numpy as np

    x = np.asarray(x)
    x_pix = np.ascontiguousarray(x.reshape(B, C, P, PXP).transpose(0, 2, 3, 1)).reshape(B, P, PXP * C)
    t = np.zeros((B, P, FIN), np.float32)
    rows = np.zeros((B, 4, 2, C, TROWS + 1, PITCH), np.float32)
    rows[:, :, :, :, 1:TROWS, 1:] = x.reshape(B, C, H // 4, 4, W // 2, 2).transpose(0, 3, 5, 1, 2, 4)
    t[:, :, 0:FIN - 1] = rows.reshape(B, P, FIN - 1)
    wf = np.concatenate([np.asarray(a).reshape(C, C, K3).transpose(2, 1, 0).reshape(K3, C * C) for a in (wr, wi)])
    small = np.ascontiguousarray(np.broadcast_to(
        np.concatenate([np.asarray(rot_b), np.asarray(gamma), np.asarray(beta)])[None, :], (P, 9)))
    w1 = np.asarray(w1)
    band = np.zeros((2, 2, 2, C, 2, 2, 2, 2, C), np.float32)
    for half in range(2):
        for r in range(2):
            for ci in range(2):
                for kind in range(2):
                    row = 2 * (half if kind == 0 else 1 - half) + 1 - r
                    for dj in range(2):
                        col = 2 * dj + 1 - ci
                        for a in range(2):
                            for e in range(2):
                                if 0 <= row - a < 3 and 0 <= col - e < 3:
                                    band[half, r, ci, :, kind, dj, a, e, :] = w1[:, :, 2 - (row - a), 2 - (col - e)].T
    return {"x_pix": x_pix, "x_tiles": t, "wf": np.ascontiguousarray(wf),
            "rotw": np.ascontiguousarray(np.asarray(rot_w).T), "small": small, "w1band": band.reshape(P, 256),
            "consts": constants()}


def kernel(x, L0_conv_w_fft_real, L0_conv_w_fft_imag, L0_conv_rot_w, L0_conv_rot_b, L0_conv_bn_gamma,
           L0_conv_bn_beta, L1_conv_weight):
    import numpy as np
    import concourse.bacc as bacc
    from concourse.bass_utils import run_bass_kernel_spmd

    arrays = lay_out(x, L0_conv_w_fft_real, L0_conv_w_fft_imag, L0_conv_rot_w, L0_conv_rot_b,
                     L0_conv_bn_gamma, L0_conv_bn_beta, L1_conv_weight)
    nc = bacc.Bacc("TRN2", target_bir_lowering=False, num_devices=1)
    args = [nc.dram_tensor(name, a.shape, F32, kind="ExternalInput").ap() for name, a in arrays.items()]
    out = nc.dram_tensor("out", (B, P, FOUT), F32, kind="ExternalOutput").ap()
    conv_program(nc, *args, out)
    got = run_bass_kernel_spmd(nc, [arrays], core_ids=[0]).results[0]["out"]
    got = got.reshape(B, 4, 2, C, TROWS, PITCH)[..., :PITCH - 1].transpose(0, 3, 4, 1, 5, 2)
    return np.ascontiguousarray(got.reshape(B, C, 4 * TROWS, W)[:, :, 2:2 + H, :])
```

```python
from contextlib import ExitStack

import concourse.bass as bass
from concourse import mybir

F32 = mybir.dt.float32
F16 = mybir.dt.float16
BF16 = mybir.dt.bfloat16
ALU = mybir.AluOpType
ACT = mybir.ActivationFunctionType
AX = mybir.AxisListType

B, C, H, W = 8, 16, 512, 512
P = 128
NPIX = H * W
GROUP = 2
K3 = 27
PITCH = W // 2 + 1
TROWS = H // 4 + 1
FOUT = TROWS * PITCH
FIN = (TROWS + 1) * PITCH + 1
BANK = 512
CB = 2
CH = CB * BANK
NFULL = FOUT // CH
NCH = NFULL + 1
TAIL = FOUT - NFULL * CH
TWIN = FIN - NFULL * CH
ROWS_CH = 4
NS = 6
RING = NS * CH
NP = 3
STEPS = 2 * NCH
THIRD = NCH // NP
AHEAD = 6
LAG = 5
HEAD = 5
SUM_LAG = 7
PRIMED = 8
LEAD = 8
GN_EPS, BN_EPS = 1e-5, 1e-5
YS = 16.0
WS = 64.0
QS = 1.0 / (2 * YS) ** 2

PXP = NPIX // P
ACHUNK = 2048
NACH = PXP * C // ACHUNK
ASLOTS = 8
AROUND = 4
ABLK = ACHUNK // P
AS = 2.0 ** -8

_COLS = [("mask_g", 128), ("fold", 16), ("gm", 128), ("rep", 128), ("pair", 16), ("id16", 16),
         ("ones", 128), ("id0", 256), ("id1", 256), ("pmask", 2), ("row0", 1), ("rown", 1),
         ("u", 9), ("v", 9), ("cm", 4), ("sm", 3)]
COL = {}
_at = 0
for _n, _w in _COLS:
    COL[_n] = (_at, _at + _w)
    _at += _w
NCONST = _at


def conv_program(nc, x_pix, x_tiles, wf, rotw, small, w1band, consts, out):
    ctx = ExitStack()
    with ctx:
        def sb(name, shape, dt=F32):
            return ctx.enter_context(nc.sbuf_tensor(name, shape, dt))

        def sem(name):
            return ctx.enter_context(nc.semaphore(name))

        img = sb("img", [P, LEAD + FIN + 1])
        nat = sb("nat", [P, 2, RING + 2], F16)
        shf = sb("shf", [P, NS, 2, CH + 2], F16)
        wc = sb("wc", [P, 2, 2, 2, 2, 64], F16)
        cst = sb("cst", [P, NCONST])
        w32 = sb("w32", [P, 256])
        w132 = sb("w132", [P, 256])
        wtmp = sb("wtmp", [P, 256])
        stats = sb("stats", [P, (CB * NFULL + 1) * 6])
        gnp = sb("gnp", [P, 4, B])
        cur = sb("cur", [P, 2, 4])
        sm = sb("sm", [P, 32])
        smallp = sb("smallp", [P, 9])
        rw = sb("rw", [C, 3])
        wfs = sb("wfs", [2 * K3, 256])
        zc = sb("zc", [P, 320])
        zt = sb("zt", [2 * K3, 9 * B])
        zu = sb("zu", [2 * K3, 9 * B])
        tapsb = sb("tapsb", [9 * B, 256])
        zero = sb("zero", [P, 16], F16)
        zerof = sb("zerof", [P, PITCH])
        eps = sb("eps", [P, 1])
        ps = ctx.enter_context(nc.psum_tensor("ps", [P, 8, 512], F32))
        ahi = nat.rearrange("p f n -> p (f n)")[:, 0:AROUND * ABLK * (P + 2)].rearrange(
            "p (s k c) -> p s k c", s=AROUND, k=ABLK)
        alo = shf.rearrange("p q f n -> p (q f n)")[:, 0:AROUND * ACHUNK].bitcast(BF16).rearrange(
            "p (s k c) -> p s k c", s=AROUND, k=ABLK)

        taps = nc.dram_tensor("taps_scratch", [B, C, 5, 5, C], F32).ap()

        o = LEAD + AHEAD * CH
        apix = img[:, o:o + ASLOTS * ACHUNK].rearrange("p (s n) -> p s n", s=ASLOTS)
        o += ASLOTS * ACHUNK
        gmask = img[:, o:o + B * P].rearrange("p (b q) -> p b q", b=B)
        o += B * P
        colsum = img[:, o:o + B]
        o += B
        gcol = img[:, o:o + 1]
        o += 1
        gtmp = img[:, o:o + P]
        o += P
        gram = img[0:C, o:o + B * C].rearrange("p (b c) -> p b c", b=B)
        o += B * C
        zpad = img[:, o:o + 400]

        def c(name, parts=P):
            a, z = COL[name]
            return cst[0:parts, a:z]

        const_in = sem("const_in")
        a_in = [sem(f"a_in{s}") for s in range(ASLOTS)]
        a_gram = sem("a_gram")
        a_hi = sem("a_hi")
        a_lo = sem("a_lo")
        a_zero = sem("a_zero")
        a_part = sem("a_part")
        a_mask = sem("a_mask")
        zpe = sem("zpe")
        zve = sem("zve")
        zac = sem("zac")
        zdma = sem("zdma")
        taps_rest = sem("taps_rest")
        dve_step = sem("dve_step")
        x_in = [sem(f"x_in{s}") for s in range(NS)]
        w_in = sem("w_in")
        cur_ready = sem("cur_ready")
        y_act = sem("y_act")
        img_wrapped = sem("img_wrapped")
        sums_done = sem("sums_done")
        upper_done = sem("upper_done")
        y_ready = sem("y_ready")
        hi_ready = sem("hi_ready")
        lo_ready = sem("lo_ready")
        shf_in = [sem(f"shf_in{s}") for s in range(NS)]
        w_ready = sem("w_ready")
        pe_done = sem("pe_done")
        evac_done = sem("evac_done")
        st_in = sem("st_in")
        st_pe = sem("st_pe")
        st_var = sem("st_var")
        st_std = sem("st_std")
        out_done = [sem(f"out_done{s}") for s in range(NP)]

        y_raw = sem("y_raw")
        lo_part = sem("lo_part")
        row_done = sem("row_done")
        col_done = sem("col_done")
        pool_step = sem("pool_step")
        passed = sem("passed")

        def hold(eng, signal, value):
            eng.wait_ge(signal, value)
            eng.sem_inc(passed, 1)

        block = ctx.enter_context(nc.Block())

        def taps_out(eng, b, signal):
            for row in range(3):
                eng.dma_start(taps[b, :, 1 + row, 1:4, :].rearrange("c q o -> q c o"),
                              tapsb[9 * b + 3 * row:9 * b + 3 * row + 3, :].rearrange("q (c o) -> q c o", c=C)
                              ).then_inc(signal, 16)

        def step(b, layer, i, r):
            return b * STEPS + layer * NCH + i * NS + r

        def ring(layer, r):
            return (layer * NCH + r) % NS

        def rounds(b, layer, i, r):
            return b * (STEPS // NS) + i + (layer * NCH + r) // NS

        def shf_count(b, layer, i, r):
            s = ring(layer, r)
            both, lower = [(n + (s == NS - 1)) * 16 for n in (2, 1)]
            used0, used1 = len(range(s, NCH, NS)), len(range((s - NCH) % NS, NCH, NS))
            first = lower if s < HEAD else both
            layer0 = first + both * (used0 - 1)
            before = b * (layer0 + lower * used1)
            k = i + r // NS
            return before + (first + both * k if layer == 0 else layer0 + lower * (k + 1))

        def upper_count(b, layer, i, r):
            return b * (HEAD + NCH) + layer * HEAD + i * NS + r + 1

        def x_count(b, i, r):
            return 16 * (b * (6 if r % NS < 3 else 5) + i + r // NS + 1)

        def by_act(r):
            return r % 3 == 2

        def width_of(n):
            return TAIL if n == NFULL else CH

        def image_after(b):
            return nc.s_assert_within(b + 1, 1, B - 1, skip_runtime_bounds_check_because="b < B - 1 here")

        def image_before(b):
            return nc.s_assert_within(b - 1, 0, B - 1, skip_runtime_bounds_check_because="b > 0 here")

        @block.sync
        def _(sp):
            for dst, src in ((cst[:, :], consts), (rw[:, :], rotw), (smallp[:, :], small),
                             (wfs[:, :], wf), (w132[:, :], w1band)):
                sp.dma_start(dst, src).then_inc(const_in, 16)
            with sp.Fori(0, B) as b:
                with sp.Fori(0, NACH // ASLOTS) as jj:
                    for s in range(ASLOTS):
                        k = b * NACH + jj * ASLOTS + s
                        hold(sp, a_lo, k + 1)
                        sp.dma_start(apix[:, s, :], x_pix[b, :, bass.ds((jj * ASLOTS + s) * ACHUNK, ACHUNK)]
                                     ).then_inc(a_in[s], 16)
            for n in range(AHEAD):
                sp.dma_start(img[:, LEAD + n * CH:LEAD + (n + 1) * CH], x_tiles[0, :, n * CH:(n + 1) * CH]
                             ).then_inc(x_in[n], 16)
            hold(sp, zve, Z_ZPAD)
            sp.dma_start(taps.rearrange("b c p q o -> (b c) (p q o)"), zpad).then_inc(zdma, 16)
            hold(sp, zdma, 16)
            hold(sp, zve, Z_TAPS)

            def load_weights(b, parts):
                for half in range(2):
                    for r in range(2):
                        if 2 * half + r not in parts:
                            continue
                        for ci in range(2):
                            g = ((half * 2 + r) * 2 + ci) * C
                            for rows, m in (((r, 4), 0),) if half == 0 else (((2 + r, 2), 0), ((r, 2), 128)):
                                sp.dma_start(w32[g:g + C, m:m + 64 * rows[1]].rearrange("c (a m) -> c a m", m=64),
                                             taps[b, :, rows[0]:rows[0] + rows[1], ci:ci + 4, :].rearrange(
                                                 "c a q o -> c a (q o)")).then_inc(w_in, 16)

            taps_out(sp, 0, zdma)
            hold(sp, zdma, 16 * 4)
            load_weights(0, range(4))

            def load_x(b, i, r, width=CH):
                hold(sp, out_done[r % NP], 16 * (b * THIRD + i * 2 + r // NP + 1))
                n = i * NS + r
                sp.dma_start(img[:, bass.ds(LEAD + n * CH, width)], x_tiles[b, :, bass.ds(n * CH, width)]
                             ).then_inc(x_in[r % NS], 16)

            def make_shifted(b, layer, i, r, last=False):
                s = ring(layer, r)
                base, width = s * CH, (TAIL if last else CH) + 1
                hold(sp, lo_ready, step(b, layer, i, r) + (1 if last else 2))
                if layer == 0 and not (type(i) is int and i == 0 and r < HEAD):
                    sp.dma_start(shf[64:128, s, :, 0:width], nat[64:128, :, base:base + width]).then_inc(shf_in[s], 16)
                cuts = [0, width] if s < NS - 1 else [0, min(CH - PITCH, width // 2 if last else CH), width]
                for a, z in zip(cuts[:-1], cuts[1:]):
                    src = (base + PITCH + a) % RING
                    sp.dma_start(shf[0:64, s, :, a:z], nat[0:64, :, src:src + z - a]).then_inc(shf_in[s], 16)

            def store(b, i, r, width=CH):
                hold(sp, evac_done, step(b, 1, i, r) + 1 + PRIMED)
                hold(sp, out_done[r % NP], 16 * (b * THIRD + i * 2 + r // NP + THIRD))
                n = i * NS + r
                sp.dma_start(out[b, :, bass.ds(n * CH, width)], img[:, bass.ds(LEAD + n * CH, width)]
                             ).then_inc(out_done[r % NP], 16)

            def store_late(b, k):
                n = NCH - LAG + k
                store(b, 0, n, width_of(n))

            with sp.Fori(0, B) as b:
                for n in range(NS):
                    make_shifted(b, 0, 0, n)
                    if n < LAG:
                        with sp.If(b > 0):
                            store_late(image_before(b), n)
                    load_x(b, 0, n + AHEAD)
                with sp.Fori(1, 4) as i:
                    for r in range(NS):
                        load_x(b, i, r + AHEAD)
                        make_shifted(b, 0, i, r)
                for n in range(24, NCH):
                    if n + AHEAD < NCH:
                        load_x(b, 0, n + AHEAD, CH if n + AHEAD < NFULL else TWIN)
                    make_shifted(b, 0, 0, n, last=(n == NFULL))
                for n in range(NS):
                    make_shifted(b, 1, 0, n)
                    if n < 4:
                        with sp.If(b < B - 1):
                            if n == 0:
                                hold(sp, w_ready, 2 * b + 2)
                                hold(sp, taps_rest, 16 * 3 * (B - 1))
                            load_weights(image_after(b), (n,))
                    if n >= LAG:
                        store(b, 0, n - LAG)
                with sp.Fori(1, 3) as i:
                    for r in range(NS):
                        make_shifted(b, 1, i, r)
                        if r >= LAG:
                            store(b, i, r - LAG)
                        else:
                            store(b, i - 1, r + NS - LAG)
                for n in range(18, NCH):
                    make_shifted(b, 1, 0, n, last=(n == NFULL))
                    store(b, 0, n - LAG)
                    if n % 2 == 0 and n < 18 + 2 * AHEAD:
                        with sp.If(b < B - 1):
                            load_x(image_after(b), 0, (n - 18) // 2)
            for k in range(LAG):
                store_late(B - 1, k)
            for r in range(NP):
                sp.wait_ge(out_done[r], 16 * (B + 1) * THIRD)

        @block.tensor
        def _(pe):
            pe.sem_inc(pe_done, NS)
            pe.sem_inc(a_gram, AROUND)
            pe.wait_ge(a_zero, 1)
            with pe.Fori(0, B // 2) as bb:
                for h in range(2):
                    b = bb * 2 + h
                    accs = [ps[:, 2 * part + h, 0:P + 1] for part in range(2)]
                    pe.wait_ge(a_mask, b + 1)
                    for acc in accs:
                        nc.tensor.matmul(acc, zerof[:, 0:P], zerof[:, 0:P + 1], start=True, stop=False)
                    with pe.Fori(0, NACH // ASLOTS) as jj:
                        for s in range(ASLOTS):
                            pe.wait_ge(a_lo, b * NACH + jj * ASLOTS + s + 1 + ASLOTS)
                            for q in range(ABLK):
                                rhs = ahi[:, s % AROUND, q, 0:P + 1]
                                nc.tensor.matmul(accs[0], ahi[:, s % AROUND, q, 0:P], rhs, start=False, stop=False)
                                mm = nc.tensor.matmul(accs[1], alo[:, s % AROUND, q, :], rhs, start=False, stop=False)
                            mm.then_inc(a_gram, 1)
                    for acc in accs:
                        mm = nc.tensor.matmul(acc, zerof[:, 0:P], zerof[:, 0:P + 1], start=False, stop=True)
                    mm.then_inc(zpe, 1)

            def mm(out_, lhs, rhs, last=True):
                m = nc.tensor.matmul(out_, lhs, rhs, start=True, stop=True)
                if last:
                    m.then_inc(zpe, 1)

            pe.wait_ge(const_in, 16 * 5)
            pe.wait_ge(zve, Z_SUMS)
            for h in range(2):
                mm(ps[0:C, 2 + h, 0:512], c("fold"), gmask[:, 4 * h:4 * h + 4, :].rearrange("p b q -> p (b q)"), False)
            mm(ps[0:C, 4, 0:B], c("fold"), colsum)
            pe.wait_ge(zve, Z_MOM)
            mm(ps[0:C, 4, 16:32], c("pair", C), zc[0:C, 0:16])
            pe.wait_ge(zve, Z_WA)
            for b in range(B):
                mm(ps[0:C, 4, 64 + 3 * b:67 + 3 * b], gram[:, b, :], zc[0:C, 72 + 3 * b:75 + 3 * b], b == B - 1)
            pe.wait_ge(zve, Z_FORMS)
            mm(ps[:, 5, 0:72], c("ones", C), zc[0:C, 96:168], False)
            mm(ps[:, 5, 128:152], c("rep", C), zc[0:C, 40:64])
            pe.wait_ge(zve, Z_T)
            mm(ps[0:9 * B, 6, 0:256], zt[:, :], wfs[:, :])


            def chunk(b, layer, i, r, width=CH, last=False):
                t = step(b, layer, i, r)
                s = ring(layer, r)
                pe.wait_ge(lo_ready, t + (1 if last else 2))
                pe.wait_ge(evac_done, t + 1 - NP + PRIMED)
                pe.wait_ge(shf_in[s], shf_count(b, layer, i, r))
                if layer == 1 or (type(i) is int and i == 0 and r < HEAD):
                    pe.wait_ge(upper_done, upper_count(b, layer, i, r))
                for q in range((width + BANK - 1) // BANK):
                    w = min(BANK, width - q * BANK)
                    k = 0
                    for whl, xhl in ((0, 0), (1, 0), (0, 1)):
                        for dj in range(2):
                            for kind in range(2):
                                at_ = q * BANK + dj
                                tiles = shf[:, s, xhl, at_:at_ + w] if kind else \
                                    nat[:, xhl, s * CH + at_:s * CH + at_ + w]
                                done = nc.tensor.matmul(
                                    ps[64 * kind:64 * kind + 64, CB * (s % NP) + q, 0:w],
                                    wc[:, layer, whl, kind, dj, :], tiles, start=(k == 0), stop=(k == 5))
                            k += 1
                done.then_inc(pe_done, 1)

            with pe.Fori(0, B) as b:
                for layer in range(2):
                    if layer == 1:
                        pe.wait_ge(st_in, b + 1)
                        nc.tensor.matmul(ps[:, 6, 0:2], c("gm"), sm[:, 2:4], start=True, stop=True).then_inc(st_pe, 1)
                    hold(pe, w_ready, 2 * b + layer + 2)
                    for r in range(NS):
                        chunk(b, layer, 0, r)
                    with pe.Fori(1, 5) as i:
                        for r in range(NS):
                            chunk(b, layer, i, r)
                    for n in range(30, NCH):
                        chunk(b, layer, 0, n, width_of(n), last=(n == NFULL))

        @block.scalar
        def _(act):
            act.sem_inc(evac_done, PRIMED)
            with act.Fori(0, B) as b:
                with act.Fori(0, NACH // ASLOTS) as jj:
                    for s in range(ASLOTS):
                        act.wait_ge(a_in[s], 16 * (b * (NACH // ASLOTS) + jj + 1))
                        act.wait_ge(a_gram, b * NACH + jj * ASLOTS + s + 1)
                        nc.scalar.activation(ahi[:, s % AROUND, :, 0:P], apix[:, s, :].rearrange("p (k c) -> p k c", c=P),
                                             ACT.Identity, scale=AS).then_inc(a_hi, 1)
            act.wait_ge(zve, Z_VAR)
            nc.scalar.activation(zc[0:C, 64:72], zc[0:C, 32:40], ACT.Sqrt).then_inc(zac, 1)
            act.wait_ge(zve, Z_BNVAR)
            nc.scalar.activation(zc[:, 176:179], zc[:, 172:175], ACT.Sqrt).then_inc(zac, 1)
            act.wait_ge(zve, Z_ANGLE)
            nc.scalar.activation(zc[:, 232:240], zc[:, 224:232], ACT.Tanh).then_inc(zac, 1)
            act.wait_ge(zve, Z_COSARG)
            nc.scalar.activation(zc[:, 248:256], zc[:, 240:248], ACT.Sin).then_inc(zac, 1)
            act.wait_ge(zve, Z_PHASE)
            nc.scalar.activation(zc[:, 272:288], zc[:, 256:272], ACT.Sin).then_inc(zac, 1)


            def y0(b, i, r, width=CH):
                if by_act(r):
                    if type(i) is int and i == 0 and r == 2:
                        act.wait_ge(cur_ready, b + 1)
                    hold(act, x_in[r % NS], x_count(b, i, r))
                    chunk = img[:, bass.ds(LEAD + (i * NS + r) * CH, width)]
                    nc.scalar.activation(chunk, chunk, ACT.Identity, bias=cur[:, 0, 3:4], scale=cur[:, 0, 1:2]
                                         ).then_inc(y_act, 1)

            def round_hi(b, layer, i, r, width=CH):
                t = step(b, layer, i, r)
                s = ring(layer, r)
                act.wait_ge(y_ready, t + 1)
                hold(act, pe_done, t + 1)
                nc.scalar.activation(nat[:, 0, s * CH:s * CH + width],
                                     img[:, bass.ds(LEAD + (i * NS + r) * CH, width)], ACT.Identity
                                     ).then_inc(hi_ready, 1)

            def evacuate(b, layer, i, r, width=CH):
                hold(act, pe_done, step(b, layer, i, r) + 1 + NS)
                at_ = CB * (ring(layer, r) % NP)
                banks = ps[:, at_:at_ + CB, :].rearrange("p a b -> p (a b)")
                nc.scalar.activation(img[:, bass.ds(LEAD + (i * NS + r) * CH, width)], banks[:, 0:width],
                                     ACT.Identity, bias=cur[:, layer, 0:1], scale=1.0 / (YS * WS)
                                     ).then_inc(evac_done, 1)

            with act.Fori(0, B) as b:
                for layer in range(2):
                    for n in range(NS):
                        if layer == 0 and n == 0:
                            y0(b, 0, 2)
                        round_hi(b, layer, 0, n)
                        if n >= LAG:
                            evacuate(b, layer, 0, n - LAG)
                        elif layer == 0:
                            with act.If(b > 0):
                                evacuate(image_before(b), 1, 0, NCH - LAG + n, width_of(NCH - LAG + n))
                        if layer == 0 and n > 0:
                            y0(b, 0, n + 2)
                    with act.Fori(1, 5) as i:
                        for r in range(NS):
                            round_hi(b, layer, i, r)
                            if r >= LAG:
                                evacuate(b, layer, i, r - LAG)
                            else:
                                evacuate(b, layer, i - 1, r + NS - LAG)
                            if layer == 0:
                                y0(b, i, r + 2)
                    for n in range(30, NCH):
                        round_hi(b, layer, 0, n, TWIN if n == NFULL else CH)
                        evacuate(b, layer, 0, n - LAG)
                        if layer == 0 and n + 2 < NCH:
                            y0(b, 0, n + 2, TWIN if n + 2 == NFULL else CH)
                    if layer == 0:
                        for n in range(NCH - LAG, NCH):
                            evacuate(b, 0, 0, n, width_of(n))
                        act.wait_ge(st_var, b + 1)
                        nc.scalar.activation(sm[:, 8:9], sm[:, 6:7], ACT.Sqrt, bias=eps[:, 0:1], scale=-QS
                                             ).then_inc(st_std, 1)
            for n in range(NCH - LAG, NCH):
                evacuate(B - 1, 1, 0, n, width_of(n))

        @block.gpsimd
        def _(pool):
            G = nc.gpsimd
            img_rows = img[:, LEAD:LEAD + TROWS * PITCH].rearrange("p (r s) -> p r s", s=PITCH)
            early = (NFULL - 1) * CH // PITCH

            def wrap(b, k, a, z):
                G.tensor_tensor(z, a, z, ALU.add).then_inc(pool_step, 1)
                hold(pool, pool_step, 6 * b + 2 * k + 1)
                return G.tensor_copy(a, z)

            pool.wait_ge(zve, Z_TAPS)
            pool.wait_ge(zdma, 16)
            for b in range(1, B):
                taps_out(pool, b, taps_rest)
            with pool.Fori(0, B) as b:
                for k, (lo, hi) in enumerate(((0, early), (early, TROWS))):
                    pool.wait_ge(sums_done, 2 * b + k + 1)
                    wrap(b, k, img_rows[:, lo:hi, 0], img_rows[:, lo:hi, PITCH - 1]).then_inc(pool_step, 1)
                pool.wait_ge(pool_step, 6 * b + 4)
                wrap(b, 2, img_rows[:, 0, :], img_rows[:, TROWS - 1, :]).then_inc(pool_step, 1)
                pool.wait_ge(pool_step, 6 * b + 6)
                pool.sem_inc(img_wrapped, 1)

        @block.vector
        def _(ve):
            V = nc.vector
            ve.sem_inc(a_lo, ASLOTS)
            ve.sem_inc(a_mask, 2)
            ve.sem_inc(w_ready, 1)
            for r in range(NP):
                ve.sem_inc(out_done[r], 16 * THIRD)
            V.memset(zero[:, :], 0.0)
            V.memset(ahi[:, :, :, P:P + 1], 1.0)
            V.memset(zerof[:, :], 0.0).then_inc(a_zero, 1)
            V.memset(img[:, 0:LEAD], 0.0).then_inc(dve_step, 1)
            V.memset(eps[:, :], GN_EPS * QS).then_inc(dve_step, 1)
            ve.wait_ge(const_in, 16 * 5)
            with ve.Fori(0, B // 2) as bb:
                for h in range(2):
                    b = bb * 2 + h
                    with ve.Fori(0, NACH // ASLOTS) as jj:
                        for s in range(ASLOTS):
                            ve.wait_ge(a_hi, b * NACH + jj * ASLOTS + s + 1)
                            V.scalar_tensor_tensor(alo[:, s % AROUND, :, :], apix[:, s, :].rearrange("p (k c) -> p k c", c=P),
                                                   AS, ahi[:, s % AROUND, :, 0:P], ALU.mult, ALU.subtract).then_inc(a_lo, 1)
                    ve.wait_ge(zpe, b + 1)
                    V.tensor_copy(gtmp, ps[:, h, 0:P]).then_inc(a_part, 1)
                    V.tensor_copy(gcol[:, 0:1], ps[:, h, P:P + 1]).then_inc(a_part, 1)
                    ve.wait_ge(a_part, 3 * b + 2)
                    V.scalar_tensor_tensor(gtmp, ps[:, 2 + h, 0:P], 2.0, gtmp, ALU.mult, ALU.add).then_inc(a_part, 1)
                    V.tensor_tensor(colsum[:, bass.ds(b, 1)], ps[:, 2 + h, P:P + 1], gcol[:, 0:1], ALU.add)
                    hold(ve, a_part, 3 * b + 3)
                    V.tensor_tensor(gmask[:, bass.ds(b, 1), :].rearrange("p b q -> p (b q)"), gtmp,
                                    c("mask_g"), ALU.mult).then_inc(a_mask, 1)

            count = [0]

            def link(ins):
                count[0] += 1
                ins.then_inc(zve, 1)
                ve.wait_ge(zve, count[0])
                return count[0]

            pe_steps = [B]
            act_steps = [0]

            def after_pe():
                pe_steps[0] += 1
                ve.wait_ge(zpe, pe_steps[0])

            def after_act():
                act_steps[0] += 1
                ve.wait_ge(zac, act_steps[0])

            def at(k, n):
                assert k == n, (k, n)

            link(V.memset(zpad, 0.0))
            ve.wait_ge(a_mask, B + 2)
            at(link(V.tensor_scalar(colsum, colsum, 1.0 / (AS * NPIX), None, ALU.mult)), Z_SUMS)
            after_pe()
            for hh in range(2):
                link(V.tensor_reduce(gram[:, 4 * hh:4 * hh + 4, :],
                                     ps[0:C, 2 + hh, :].rearrange("p (b k c) -> p b c k", b=4, k=8),
                                     AX.X, ALU.add))
            link(V.tensor_scalar(gram, gram, 1.0 / (AS * AS * NPIX), None, ALU.mult))
            link(V.tensor_copy(zc[0:C, 0:8], ps[0:C, 4, 0:8]))
            diag = wtmp[0:C, 0:B * C].rearrange("p (b c) -> p b c", b=B)
            link(V.tensor_tensor(diag, gram, c("id16", C).unsqueeze(1).to_broadcast([C, B, C]), ALU.mult))
            n = link(V.tensor_reduce(zc[0:C, 8:16], diag, AX.X, ALU.add))
            at(n, Z_MOM)
            after_pe()
            gmean, var, std, inv = zc[0:C, 40:48], zc[0:C, 32:40], zc[0:C, 64:72], zc[0:C, 16:24]
            tmp = zc[0:C, 24:32]
            link(V.tensor_copy(gmean, ps[0:C, 4, 16:24]))
            link(V.tensor_tensor(tmp, gmean, gmean, ALU.mult))
            link(V.tensor_tensor(var, ps[0:C, 4, 24:32], tmp, ALU.subtract))
            at(link(V.tensor_scalar(var, var, GN_EPS, None, ALU.add)), Z_VAR)

            def newton(inv, std, var, tmp):
                link(V.reciprocal(inv, std))
                link(V.tensor_tensor(tmp, inv, inv, ALU.mult))
                link(V.tensor_tensor(tmp, tmp, var, ALU.mult))
                link(V.tensor_scalar(tmp, tmp, -0.5, 1.5, ALU.mult, ALU.add))
                link(V.tensor_tensor(inv, inv, tmp, ALU.mult))

            after_act()
            newton(inv, std, var, tmp)
            link(V.tensor_scalar(zc[0:C, 48:56], inv, YS, None, ALU.mult))
            link(V.tensor_tensor(tmp, inv, var, ALU.mult))
            link(V.tensor_scalar(zc[0:C, 56:64], tmp, WS, None, ALU.mult))
            wa = zc[0:C, 72:96].rearrange("p (b o) -> p b o", o=3)
            for k in range(3):
                n = link(V.tensor_scalar(wa[:, :, k], inv, rw[:, k:k + 1], None, ALU.mult))
            at(n, Z_WA)
            forms = zc[0:C, 96:168].rearrange("p (f b o) -> p f b o", f=3, o=3)
            link(V.tensor_tensor(tmp, zc[0:C, 0:8], gmean, ALU.subtract))
            for k in range(3):
                link(V.tensor_tensor(forms[:, 1, :, k], wa[:, :, k], zc[0:C, 0:8], ALU.mult))
                link(V.tensor_tensor(forms[:, 2, :, k], wa[:, :, k], tmp, ALU.mult))
            after_pe()
            at(link(V.tensor_tensor(zc[0:C, 96:120], zc[0:C, 72:96], ps[0:C, 4, 64:88], ALU.mult)), Z_FORMS)
            after_pe()
            q = zc[:, 96:168]
            link(V.tensor_copy(q, ps[:, 5, 0:72]))
            link(V.tensor_copy(gnp[:, 0:3, :], ps[:, 5, 128:152].rearrange("p (f b) -> p f b", f=3)))
            link(V.scalar_tensor_tensor(gnp[:, 3, :], gnp[:, 0, :], -1.0, gnp[:, 1, :], ALU.mult, ALU.mult))
            qz, qm, qs = q[:, 0:24], q[:, 24:48], q[:, 48:72]

            def bo(a):
                return a.rearrange("p (b o) -> p b o", o=3)

            def ob(a):
                return a.rearrange("p (b o) -> p o b", o=3)

            link(V.tensor_tensor(qm, qm, qm, ALU.mult))
            link(V.tensor_tensor(qz, qz, qm, ALU.subtract))
            for k in range(3):
                link(V.tensor_scalar(bo(qs)[:, :, k], bo(qs)[:, :, k], smallp[:, k:k + 1], None, ALU.add))
            zm = zc[:, 168:171]
            link(V.tensor_reduce(zm, ob(qs), AX.X, ALU.add))
            link(V.tensor_scalar(zm, zm, 1.0 / B, None, ALU.mult))
            for k in range(3):
                link(V.tensor_scalar(bo(qs)[:, :, k], bo(qs)[:, :, k], zm[:, k:k + 1], None, ALU.subtract))
            link(V.tensor_tensor(qm, qs, qs, ALU.mult))
            link(V.tensor_tensor(qz, qz, qm, ALU.add))
            bv = zc[:, 172:175]
            link(V.tensor_reduce(bv, ob(qz), AX.X, ALU.add))
            at(link(V.tensor_scalar(bv, bv, 1.0 / B, BN_EPS, ALU.mult, ALU.add)), Z_BNVAR)
            after_act()
            bi = zc[:, 180:183]
            newton(bi, zc[:, 176:179], bv, zc[:, 184:187])
            link(V.tensor_tensor(bi, bi, smallp[:, 3:6], ALU.mult))
            for k in range(3):
                link(V.tensor_scalar(bo(qs)[:, :, k], bo(qs)[:, :, k], bi[:, k:k + 1], smallp[:, 6 + k:7 + k],
                                     ALU.mult, ALU.add))
            at(link(V.tensor_reduce(zc[:, 224:232], bo(qs), AX.X, ALU.add)), Z_ANGLE)
            after_act()
            pi = 3.141592653589793
            at(link(V.tensor_scalar(zc[:, 240:248], zc[:, 232:240], pi / 4, pi / 2, ALU.mult, ALU.add)), Z_COSARG)
            after_act()
            link(V.tensor_scalar(zc[:, 256:264], zc[:, 248:256], 2 * pi / 3, None, ALU.mult))
            at(link(V.tensor_scalar(zc[:, 264:272], zc[:, 248:256], -2 * pi / 3, pi / 2, ALU.mult, ALU.add)), Z_PHASE)
            after_act()
            s1, c1 = zc[:, 272:280], zc[:, 280:288]
            s2, c2, s3, c3 = zc[:, 192:200], zc[:, 200:208], zc[:, 208:216], zc[:, 216:224]
            t8 = zc[:, 288:296]
            link(V.tensor_tensor(s2, s1, c1, ALU.mult))
            link(V.tensor_scalar(s2, s2, 2.0, None, ALU.mult))
            link(V.tensor_tensor(c2, c1, c1, ALU.mult))
            link(V.tensor_scalar(c2, c2, 2.0, -1.0, ALU.mult, ALU.add))
            link(V.tensor_tensor(s3, s2, c1, ALU.mult))
            link(V.tensor_tensor(t8, c2, s1, ALU.mult))
            link(V.tensor_tensor(s3, s3, t8, ALU.add))
            link(V.tensor_tensor(c3, c2, c1, ALU.mult))
            link(V.tensor_tensor(t8, s2, s1, ALU.mult))
            link(V.tensor_tensor(c3, c3, t8, ALU.subtract))
            n2 = 2 * K3
            cf, sf = zc[0:n2, 96:104], zc[0:n2, 104:112]
            cm, smk = c("cm", n2), c("sm", n2)
            link(V.tensor_scalar(cf, c1[0:n2, :], cm[:, 1:2], cm[:, 0:1], ALU.mult, ALU.add))
            link(V.scalar_tensor_tensor(cf, c2[0:n2, :], cm[:, 2:3], cf, ALU.mult, ALU.add))
            link(V.scalar_tensor_tensor(cf, c3[0:n2, :], cm[:, 3:4], cf, ALU.mult, ALU.add))
            link(V.tensor_scalar(sf, s1[0:n2, :], smk[:, 0:1], None, ALU.mult))
            link(V.scalar_tensor_tensor(sf, s2[0:n2, :], smk[:, 1:2], sf, ALU.mult, ALU.add))
            link(V.scalar_tensor_tensor(sf, s3[0:n2, :], smk[:, 2:3], sf, ALU.mult, ALU.add))
            ztb, zub = (a.rearrange("p (b t) -> p b t", t=9) for a in (zt, zu))

            def by_image(a):
                return a.unsqueeze(2).to_broadcast([n2, B, 9])

            def by_tap(a):
                return a.unsqueeze(1).to_broadcast([n2, B, 9])

            link(V.tensor_tensor(ztb, by_image(cf), by_tap(c("u", n2)), ALU.mult))
            link(V.tensor_tensor(zub, by_image(sf), by_tap(c("v", n2)), ALU.mult))
            n = link(V.tensor_tensor(ztb, ztb, zub, ALU.add))
            at(n, Z_T)
            after_pe()
            at(link(V.tensor_copy(tapsb[:, :], ps[0:9 * B, 6, 0:256])), Z_TAPS)
            V.tensor_scalar(w132[:, :], w132[:, :], WS, None, ALU.mult).then_inc(dve_step, 1)


            PER_IMAGE = 3 + 1 + 2 + 3 + 1 + 3
            mark = [0]

            def chain(ins, b):
                mark[0] += 1
                ins.then_inc(dve_step, 1)
                ve.wait_ge(dve_step, b * PER_IMAGE + mark[0] + 3)

            def weights(b, layer, w):
                chain(V.scalar_tensor_tensor(wtmp[:, :], c("id0" if layer == 0 else "id1"), cur[:, layer, 2:3], w,
                                             ALU.mult, ALU.add), b)
                for kind in range(2):
                    src = wtmp[:, 128 * kind:128 * kind + 128].rearrange("p (a d m) -> p a d m", a=2, d=2)
                    hi, lo = [wc[:, layer, part, kind].rearrange("p d (a m) -> p a d m", a=2) for part in range(2)]
                    chain(V.tensor_copy(hi, src), b)
                    ins = V.tensor_tensor(lo, src, hi, ALU.subtract)
                ins.then_inc(w_ready, 1)

            def normalize(dst, src, layer):
                return V.tensor_scalar(dst, src, cur[:, layer, 0:1], cur[:, layer, 1:2], ALU.subtract, ALU.mult)

            def split_lo(b, layer, i, r, width=CH):
                s = ring(layer, r)
                ve.wait_ge(hi_ready, step(b, layer, i, r) + 1)
                lo = V.tensor_tensor(nat[:, 1, s * CH:s * CH + width],
                                     img[:, bass.ds(LEAD + (i * NS + r) * CH, width)],
                                     nat[:, 0, s * CH:s * CH + width], ALU.subtract)
                if s == 0:
                    lo.then_inc(lo_part, 1)
                    ve.wait_ge(lo_part, rounds(b, layer, i, r) + 1)
                    V.tensor_copy(nat[:, :, RING:RING + 1], nat[:, :, 0:1]).then_inc(lo_ready, 1)
                else:
                    lo.then_inc(lo_ready, 1)

            def y0(b, i, r, width=CH):
                if by_act(r):
                    return
                ve.wait_ge(x_in[r % NS], x_count(b, i, r))
                chunk = img[:, bass.ds(LEAD + (i * NS + r) * CH, width)]
                normalize(chunk, chunk, 0).then_inc(y_raw, 1)

            def zero_edge(b, i, r, last=False):
                n = i * NS + r
                rows = 3 if last else ROWS_CH
                if by_act(r):
                    ve.wait_ge(y_act, b * THIRD + i * 2 + r // 3 + 1)
                else:
                    ve.wait_ge(y_raw, 2 * (b * THIRD + i * 2 + r // 3) + r % 3 + 1)
                if type(n) is int and n == 0:
                    V.tensor_copy(img[:, LEAD + 1:LEAD + PITCH], zerof[:, 1:PITCH])
                if last:
                    V.tensor_copy(img[:, LEAD + FOUT + 1:LEAD + FOUT + PITCH], zerof[:, 1:PITCH])
                edge = img[:, bass.ds(LEAD + n * (ROWS_CH * PITCH), (rows - 1) * PITCH + 1)]
                V.tensor_copy(edge[:, 0:(rows - 1) * PITCH + 1:PITCH], zero[:, 0:rows]).then_inc(y_ready, 1)

            def mask_row(b, first):
                at_ = LEAD + (0 if first else FOUT - PITCH)
                V.tensor_scalar(img[:, at_:at_ + PITCH], img[:, at_:at_ + PITCH],
                                c("row0" if first else "rown"), None, ALU.mult).then_inc(row_done, 1)
                hold(ve, row_done, 2 * b + (1 if first else 2))

            def mask_columns(b, i, r, last=False):
                ve.wait_ge(evac_done, step(b, 0, i, r) + 1 + PRIMED)
                if last:
                    mask_row(b, False)
                rows = 2 if last else ROWS_CH
                pairs = img[:, bass.ds(LEAD - 1 + (i * NS + r) * (ROWS_CH * PITCH), rows * PITCH)].rearrange(
                    "p (k s) -> p k s", s=PITCH)[:, :, 0:2]
                V.tensor_tensor(pairs, pairs, c("pmask").unsqueeze(1).to_broadcast([P, rows, 2]),
                                ALU.mult).then_inc(col_done, 1)

            def sum_x1(b, i, r, width=CH):
                n = i * NS + r
                ve.wait_ge(col_done, b * NCH + n + 1)
                for k in range((width + BANK - 1) // BANK):
                    w = min(BANK, width - BANK * k)
                    ins = V.bn_stats(stats[:, bass.ds((n * CB + k) * 6, 6)],
                                     img[:, bass.ds(LEAD + n * CH + BANK * k, w)])
                return ins

            def y1(b, i, r, width=CH):
                chunk = img[:, bass.ds(LEAD + (i * NS + r) * CH, width)]
                normalize(chunk, chunk, 1).then_inc(y_ready, 1)

            def copy_upper(b, layer, i, r, width=CH, last=False):
                s = ring(layer, r)
                ve.wait_ge(lo_ready, step(b, layer, i, r) + (1 if last else 2))
                V.tensor_copy(shf[64:128, s, :, 0:width + 1], nat[64:128, :, s * CH:s * CH + width + 1]
                              ).then_inc(upper_done, 1)

            def step0(b, i, r, last=False):
                mask_columns(b, i, r - SUM_LAG)
                y0(b, i, r, TWIN if last else CH)
                sum_x1(b, i, r - SUM_LAG)
                zero_edge(b, i, r, last)
                split_lo(b, 0, i, r - 1)

            with ve.Fori(0, B) as b:
                mark[0] = 0
                V.tensor_copy(cur[:, 0, :], gnp[:, :, bass.ds(b, 1)].rearrange("p f b -> p (f b)")
                              ).then_inc(cur_ready, 1)
                ve.wait_ge(cur_ready, b + 1)
                for n in range(SUM_LAG):
                    y0(b, 0, n)
                    if n > 0:
                        split_lo(b, 0, 0, n - 1)
                    zero_edge(b, 0, n)
                    if n >= 2:
                        copy_upper(b, 0, 0, n - 2)
                    if n == 1:
                        ve.wait_ge(w_in, 16 * 12 * (b + 1))
                        weights(b, 0, w32[:, :])
                ve.wait_ge(evac_done, step(b, 0, 0, 0) + 1 + PRIMED)
                mask_row(b, True)
                with ve.Fori(0, 4) as i:
                    for r in range(SUM_LAG, SUM_LAG + NS):
                        step0(b, i, r)
                step0(b, 0, 31)
                step0(b, 0, 32, last=True)
                split_lo(b, 0, 0, NFULL, TWIN)
                for n in range(NCH - SUM_LAG, NFULL - 1):
                    mask_columns(b, 0, n)
                    ins = sum_x1(b, 0, n)
                ins.then_inc(sums_done, 1)
                mask_columns(b, 0, NFULL - 1)
                sum_x1(b, 0, NFULL - 1)
                mask_columns(b, 0, NFULL, last=True)
                sum_x1(b, 0, NFULL, TAIL).then_inc(sums_done, 1)

                hold(ve, sums_done, 2 * b + 2)
                chain(V.bn_aggr(sm[:, 2:4], stats[:, :]), b)
                V.scalar_tensor_tensor(sm[:, 3:4], sm[:, 2:3], sm[:, 2:3], sm[:, 3:4], ALU.mult, ALU.add
                                       ).then_inc(st_in, 1)
                mean, neg, var, q, inv, two_q = cur[:, 1, 0:1], sm[:, 6:7], sm[:, 7:8], sm[:, 8:9], sm[:, 9:10], sm[:, 10:11]
                ve.wait_ge(st_pe, b + 1)
                chain(V.tensor_copy(mean, ps[:, 6, 0:1]), b)
                V.scalar_tensor_tensor(neg, mean, mean, ps[:, 6, 1:2], ALU.mult, ALU.subtract).then_inc(st_var, 1)
                ve.wait_ge(st_var, b + 1)
                chain(V.tensor_scalar(var, neg, -QS, GN_EPS * QS, ALU.mult, ALU.add), b)
                ve.wait_ge(st_std, b + 1)
                chain(V.reciprocal(inv, q), b)
                chain(V.scalar_tensor_tensor(two_q, inv, var, q, ALU.mult, ALU.add), b)
                chain(V.reciprocal(cur[:, 1, 1:2], two_q), b)
                ve.wait_ge(img_wrapped, b + 1)
                y1(b, 0, 0)
                y1(b, 0, 1)
                split_lo(b, 1, 0, 0)
                split_lo(b, 1, 0, 1)
                chain(V.tensor_scalar(cur[:, 1, 2:3], two_q, YS * WS, None, ALU.mult), b)
                weights(b, 1, w132[:, :])
                y1(b, 0, 2)
                copy_upper(b, 1, 0, 0)
                y1(b, 0, 3)
                per_image = mark[0]
                for n in range(2, NS):
                    split_lo(b, 1, 0, n)
                    y1(b, 0, n + 2)
                    copy_upper(b, 1, 0, n - 1)
                with ve.Fori(1, 5) as i:
                    for r in range(NS):
                        split_lo(b, 1, i, r)
                        y1(b, i, r + 2)
                        copy_upper(b, 1, i, r - 1)
                split_lo(b, 1, 0, 30)
                y1(b, 0, NFULL, TWIN)
                copy_upper(b, 1, 0, 29)
                for n in (31, 32):
                    split_lo(b, 1, 0, n, TWIN if n == NFULL else CH)
                    copy_upper(b, 1, 0, n - 1)
                copy_upper(b, 1, 0, NFULL, TAIL, last=True)
            assert per_image == PER_IMAGE, (per_image, PER_IMAGE)


Z_ZPAD = 1
Z_SUMS = 2
Z_MOM = Z_SUMS + 4 + 2
Z_VAR = Z_MOM + 4
Z_WA = Z_VAR + 5 + 3 + 3
Z_FORMS = Z_WA + 1 + 6 + 1
Z_BNVAR = Z_FORMS + 3 + 2 + 3 + 2 + 3 + 2 + 2
Z_ANGLE = Z_BNVAR + 5 + 1 + 3 + 1
Z_COSARG = Z_ANGLE + 1
Z_PHASE = Z_COSARG + 2
Z_T = Z_PHASE + 10 + 6 + 3
Z_TAPS = Z_T + 1


def row_first(band):
    import numpy as np

    return np.ascontiguousarray(band.reshape(P, 2, 2, 2, 32).transpose(0, 1, 3, 2, 4)).reshape(P, 256)


def constants():
    import numpy as np

    k = np.zeros((P, NCONST), np.float32)

    def put(name, a):
        lo, hi = COL[name]
        a = np.asarray(a, np.float32)
        k[0:a.shape[0], lo:hi] = a.reshape(a.shape[0], hi - lo)

    p = np.arange(P)
    ch = p % C
    put("mask_g", (p[:, None] // C) == (p[None, :] // C))
    put("fold", ch[:, None] == np.arange(C)[None, :])
    put("gm", (ch[:, None] // GROUP == ch[None, :] // GROUP) * (FOUT / (GROUP * NPIX)))
    put("rep", np.arange(C)[:, None] == ch[None, :])
    c16 = np.arange(C)
    put("pair", (c16[:, None] // GROUP == c16[None, :] // GROUP) / GROUP)
    put("id16", np.eye(C))
    put("ones", np.ones((P, P)))
    half, r, ci = p // 64, p // 32 % 2, p // 16 % 2
    id0, id1 = np.zeros((P, 2, 2, 64)), np.zeros((P, 2, 2, 64))
    for kind in range(2):
        rows0 = 2 * (half if kind == 0 else 1 - half) + r
        rows1 = 2 * (half if kind == 0 else 1 - half) + 1 - r
        for dj in range(2):
            for m in range(64):
                a, e, o_ = m // 32, m // 16 % 2, m % 16
                id0[:, kind, dj, m] = (ch == o_) & (rows0 == 2 - a) & (2 * dj + ci == 2 - e)
                id1[:, kind, dj, m] = (ch == o_) & (rows1 == 1 + a) & (2 * dj + 1 - ci == 1 + e)
    put("id0", row_first(id0))
    put("id1", row_first(id1))
    put("pmask", np.stack([ci == 1, ci == 0], 1))
    put("row0", (half == 1) & (r == 0))
    put("rown", ~((half == 1) & (r == 0)))
    f = np.array([0, 1, -1])
    f1, f2, f3 = (a.ravel() for a in np.meshgrid(f, f, f, indexing="ij"))
    fs = f1 + f2 + f3
    pp, qq = np.meshgrid(np.arange(3), np.arange(3), indexing="ij")
    ang = 2 * np.pi / 3 * (f1[:, None] + f2[:, None] * pp.ravel() + f3[:, None] * qq.ravel())
    g = WS / K3
    put("u", np.concatenate([np.cos(ang), -np.sin(ang)]) * g)
    put("v", np.concatenate([np.sin(ang), np.cos(ang)]) * g)
    put("cm", np.tile(np.abs(fs)[:, None] == np.arange(4), (2, 1)))
    put("sm", np.tile((np.abs(fs)[:, None] == np.arange(1, 4)) * np.sign(fs)[:, None], (2, 1)))
    return k


def lay_out(x, wr, wi, rot_w, rot_b, gamma, beta, w1):
    import numpy as np

    x = np.asarray(x)
    x_pix = np.ascontiguousarray(x.reshape(B, C, P, PXP).transpose(0, 2, 3, 1)).reshape(B, P, PXP * C)
    t = np.zeros((B, P, FIN), np.float32)
    rows = np.zeros((B, 4, 2, C, TROWS + 1, PITCH), np.float32)
    rows[:, :, :, :, 1:TROWS, 1:] = x.reshape(B, C, H // 4, 4, W // 2, 2).transpose(0, 3, 5, 1, 2, 4)
    t[:, :, 0:FIN - 1] = rows.reshape(B, P, FIN - 1)
    wf = np.concatenate([np.asarray(a).reshape(C, C, K3).transpose(2, 1, 0).reshape(K3, C * C) for a in (wr, wi)])
    small = np.ascontiguousarray(np.broadcast_to(
        np.concatenate([np.asarray(rot_b), np.asarray(gamma), np.asarray(beta)])[None, :], (P, 9)))
    w1 = np.asarray(w1)
    band = np.zeros((2, 2, 2, C, 2, 2, 2, 2, C), np.float32)
    for half in range(2):
        for r in range(2):
            for ci in range(2):
                for kind in range(2):
                    row = 2 * (half if kind == 0 else 1 - half) + 1 - r
                    for dj in range(2):
                        col = 2 * dj + 1 - ci
                        for a in range(2):
                            for e in range(2):
                                if 0 <= row - a < 3 and 0 <= col - e < 3:
                                    band[half, r, ci, :, kind, dj, a, e, :] = w1[:, :, 2 - (row - a), 2 - (col - e)].T
    return {"x_pix": x_pix, "x_tiles": t, "wf": np.ascontiguousarray(wf),
            "rotw": np.ascontiguousarray(np.asarray(rot_w).T), "small": small, "w1band": row_first(band),
            "consts": constants()}


def kernel(x, L0_conv_w_fft_real, L0_conv_w_fft_imag, L0_conv_rot_w, L0_conv_rot_b, L0_conv_bn_gamma,
           L0_conv_bn_beta, L1_conv_weight):
    import numpy as np
    import concourse.bacc as bacc
    from concourse.bass_utils import run_bass_kernel_spmd

    arrays = lay_out(x, L0_conv_w_fft_real, L0_conv_w_fft_imag, L0_conv_rot_w, L0_conv_rot_b,
                     L0_conv_bn_gamma, L0_conv_bn_beta, L1_conv_weight)
    nc = bacc.Bacc("TRN2", target_bir_lowering=False, num_devices=1)
    args = [nc.dram_tensor(name, a.shape, F32, kind="ExternalInput").ap() for name, a in arrays.items()]
    out = nc.dram_tensor("out", (B, P, FOUT), F32, kind="ExternalOutput").ap()
    conv_program(nc, *args, out)
    got = run_bass_kernel_spmd(nc, [arrays], core_ids=[0]).results[0]["out"]
    got = got.reshape(B, 4, 2, C, TROWS, PITCH)[..., :PITCH - 1].transpose(0, 3, 4, 1, 5, 2)
    return np.ascontiguousarray(got.reshape(B, C, 4 * TROWS, W)[:, :, 2:2 + H, :])
```
